# Optimizing a Trainium2 kernel written in Bass

```python
import numpy as np
import jax
import jax.numpy as jnp

def _softmax(x, axis=-1):
    return jax.nn.softmax(x, axis=axis)

def _gelu(x):
    return jax.nn.gelu(x, approximate=True)

def _silu(x):
    return jax.nn.silu(x)

def _sigmoid(x):
    return jax.nn.sigmoid(x)

def _layernorm(x, axis=-1, eps=1e-05):
    m = jnp.mean(x, axis=axis, keepdims=True)
    v = jnp.var(x, axis=axis, keepdims=True)
    return (x - m) / jnp.sqrt(v + eps)

def _scatter_add(tgt, idx, src, axis=0):
    return tgt.at[idx].add(src)

def _segment_sum(src, seg, n):
    return jax.ops.segment_sum(src, seg, n)
kernel_name = 'mk_seq_preln_d1_jaxref_r8_3b8beb'

def setup_inputs(seed: int=0):
    np.random.seed(seed)
    _w = jnp.asarray

    def _L0_attn_setup():
        import jax, jax.numpy as jnp
        import numpy as np
        D_MODEL = 512
        N_Q = 32
        N_KV = 8
        HD = 128
        SLIDE = 64

        def _gqa_swa_attention(q, k, v, slide):
            B, Hq, N, D = q.shape
            Hkv = k.shape[1]
            G = Hq // Hkv
            qg = q.reshape(B, Hkv, G, N, D)
            scale = 1.0 / jnp.sqrt(jnp.asarray(D, q.dtype))
            s = jnp.einsum('bhgnd,bhmd->bhgnm', qg, k) * scale
            i = jnp.arange(N)[:, None]
            j = jnp.arange(N)[None, :]
            mask = j <= i
            if slide > 0:
                mask = mask & (i - j < slide)
            s = jnp.where(mask[None, None, None], s, jnp.asarray(-jnp.inf, s.dtype))
            p = jax.nn.softmax(s, axis=-1)
            o = jnp.einsum('bhgnm,bhmd->bhgnd', p, v)
            return o.reshape(B, Hq, N, D)
        key = jax.random.key(seed)
        ks = jax.random.split(key, 5)
        std = 0.01
        x = jax.random.normal(ks[0], (2, 256, D_MODEL), dtype=jnp.float32)
        wq = jax.random.normal(ks[1], (N_Q * HD, D_MODEL), dtype=jnp.float32) * std
        wk = jax.random.normal(ks[2], (N_KV * HD, D_MODEL), dtype=jnp.float32) * std
        wv = jax.random.normal(ks[3], (N_KV * HD, D_MODEL), dtype=jnp.float32) * std
        wo = jax.random.normal(ks[4], (D_MODEL, N_Q * HD), dtype=jnp.float32) * std
        return {'x': x, 'wq': wq, 'wk': wk, 'wv': wv, 'wo': wo}
    _L0_attn_in = _L0_attn_setup()

    def _L0_ffn_setup():
        import jax, jax.numpy as jnp
        import numpy as np
        BLOCK = 64
        NF4_CODE = jnp.array([-1.0, -0.6961928009986877, -0.5250730514526367, -0.39491748809814453, -0.28444138169288635, -0.18477343022823334, -0.09105003625154495, 0.0, 0.07958029955625534, 0.16093020141124725, 0.24611230194568634, 0.33791524171829224, 0.44070982933044434, 0.5626170039176941, 0.7229568362236023, 1.0], dtype=jnp.float32)

        def dequant_nf4(q, absmax, shape):
            w = NF4_CODE[q.reshape(-1)]
            w = w.reshape(-1, BLOCK) * absmax[:, None]
            return w.reshape(shape)
        key = jax.random.key(seed)
        ks = jax.random.split(key, 7)
        HD, M = (512, 1792)
        nblk = HD * M // BLOCK
        x = jax.random.normal(ks[0], (2, 256, HD), dtype=jnp.float32)
        gate_q = jax.random.randint(ks[1], (M, HD), 0, 16, dtype=jnp.int32)
        up_q = jax.random.randint(ks[2], (M, HD), 0, 16, dtype=jnp.int32)
        down_q = jax.random.randint(ks[3], (HD, M), 0, 16, dtype=jnp.int32)
        gate_absmax = jax.random.uniform(ks[4], (nblk,), dtype=jnp.float32) * 0.05
        up_absmax = jax.random.uniform(ks[5], (nblk,), dtype=jnp.float32) * 0.05
        down_absmax = jax.random.uniform(ks[6], (nblk,), dtype=jnp.float32) * 0.05
        return {'x': x, 'gate_q': gate_q, 'gate_absmax': gate_absmax, 'up_q': up_q, 'up_absmax': up_absmax, 'down_q': down_q, 'down_absmax': down_absmax}
    _L0_ffn_in = _L0_ffn_setup()
    _d = {'L0_attn_x': _L0_attn_in['x'], 'L0_attn_wq': _L0_attn_in['wq'], 'L0_attn_wk': _L0_attn_in['wk'], 'L0_attn_wv': _L0_attn_in['wv'], 'L0_attn_wo': _L0_attn_in['wo'], 'L0_ffn_gate_q': _L0_ffn_in['gate_q'], 'L0_ffn_gate_absmax': _L0_ffn_in['gate_absmax'], 'L0_ffn_up_q': _L0_ffn_in['up_q'], 'L0_ffn_up_absmax': _L0_ffn_in['up_absmax'], 'L0_ffn_down_q': _L0_ffn_in['down_q'], 'L0_ffn_down_absmax': _L0_ffn_in['down_absmax']}
    _x0 = _d['L0_attn_x']
    _d['L0_attn_x'] = jax.random.normal(jax.random.fold_in(jax.random.key(seed), 1), (2, 1024, 512), dtype=_x0.dtype)
    del _x0
    return _d

def reference(L0_attn_x, L0_attn_wq, L0_attn_wk, L0_attn_wv, L0_attn_wo, L0_ffn_gate_q, L0_ffn_gate_absmax, L0_ffn_up_q, L0_ffn_up_absmax, L0_ffn_down_q, L0_ffn_down_absmax):

    def _L0_attn_ref(x, wq, wk, wv, wo):
        import jax, jax.numpy as jnp
        import numpy as np
        D_MODEL = 512
        N_Q = 32
        N_KV = 8
        HD = 128
        SLIDE = 64

        def _gqa_swa_attention(q, k, v, slide):
            B, Hq, N, D = q.shape
            Hkv = k.shape[1]
            G = Hq // Hkv
            qg = q.reshape(B, Hkv, G, N, D)
            scale = 1.0 / jnp.sqrt(jnp.asarray(D, q.dtype))
            s = jnp.einsum('bhgnd,bhmd->bhgnm', qg, k) * scale
            i = jnp.arange(N)[:, None]
            j = jnp.arange(N)[None, :]
            mask = j <= i
            if slide > 0:
                mask = mask & (i - j < slide)
            s = jnp.where(mask[None, None, None], s, jnp.asarray(-jnp.inf, s.dtype))
            p = jax.nn.softmax(s, axis=-1)
            o = jnp.einsum('bhgnm,bhmd->bhgnd', p, v)
            return o.reshape(B, Hq, N, D)
        B, N, _ = x.shape
        q = (x @ wq.T).reshape(B, N, N_Q, HD).transpose(0, 2, 1, 3)
        k = (x @ wk.T).reshape(B, N, N_KV, HD).transpose(0, 2, 1, 3)
        v = (x @ wv.T).reshape(B, N, N_KV, HD).transpose(0, 2, 1, 3)
        o = _gqa_swa_attention(q, k, v, SLIDE)
        o = o.transpose(0, 2, 1, 3).reshape(B, N, N_Q * HD)
        return o @ wo.T

    def _L0_ffn_ref(x, gate_q, gate_absmax, up_q, up_absmax, down_q, down_absmax):
        import jax, jax.numpy as jnp
        import numpy as np
        BLOCK = 64
        NF4_CODE = jnp.array([-1.0, -0.6961928009986877, -0.5250730514526367, -0.39491748809814453, -0.28444138169288635, -0.18477343022823334, -0.09105003625154495, 0.0, 0.07958029955625534, 0.16093020141124725, 0.24611230194568634, 0.33791524171829224, 0.44070982933044434, 0.5626170039176941, 0.7229568362236023, 1.0], dtype=jnp.float32)

        def dequant_nf4(q, absmax, shape):
            w = NF4_CODE[q.reshape(-1)]
            w = w.reshape(-1, BLOCK) * absmax[:, None]
            return w.reshape(shape)
        HD = x.shape[-1]
        M = gate_q.shape[0]
        Wg = dequant_nf4(gate_q, gate_absmax, (M, HD))
        Wu = dequant_nf4(up_q, up_absmax, (M, HD))
        Wd = dequant_nf4(down_q, down_absmax, (HD, M))
        g = jnp.einsum('bsh,mh->bsm', x, Wg)
        u = jnp.einsum('bsh,mh->bsm', x, Wu)
        h = jax.nn.silu(g) * u
        return jnp.einsum('bsm,hm->bsh', h, Wd)
    x = L0_attn_x
    x = x + _L0_attn_ref(_layernorm(x, axis=-1), L0_attn_wq, L0_attn_wk, L0_attn_wv, L0_attn_wo)
    x = x + _L0_ffn_ref(_layernorm(x, axis=-1), L0_ffn_gate_q, L0_ffn_gate_absmax, L0_ffn_up_q, L0_ffn_up_absmax, L0_ffn_down_q, L0_ffn_down_absmax)
    return x

_drawn_inputs = setup_inputs


def setup_inputs(seed=0):
    import zlib

    import numpy as np

    out = dict(_drawn_inputs(seed))
    spreads = {}
    factors = {'L0_attn_wq': 8.0,
     'L0_attn_wk': 8.0,
     'L0_attn_wv': 2.815,
     'L0_attn_wo': 2.8,
     'L0_ffn_gate_absmax': 3.003,
     'L0_ffn_up_absmax': 3.027,
     'L0_ffn_down_absmax': 3.027}
    for name, (base, spread) in spreads.items():
        noise = np.random.default_rng([zlib.crc32(name.encode()), seed]).standard_normal(out[name].shape)
        drawn = base * np.exp(spread * noise) if base else spread * noise
        out[name] = jnp.asarray(drawn.astype(out[name].dtype))
    for name, factor in factors.items():
        out[name] = (out[name] * factor).astype(out[name].dtype)
    return out
```

```python
from contextlib import ExitStack

import concourse.bass as bass
import concourse.mybir as mybir
import numpy as np

F32 = mybir.dt.float32
F32R = mybir.dt.float32r
I32 = mybir.dt.int32
ALU = mybir.AluOpType
ACT = mybir.ActivationFunctionType
AX = mybir.AxisListType

P = 128
BATCH, SEQ, D = 2, 1024, 512
N_KV, GROUP, HD, WINDOW = 8, 4, 128, 64
M_FFN, QBLOCK = 1792, 64
EPS = 1e-5
SCALE = float(HD) ** -0.5
MASKED = -1.0e30

KC = D // P
STEP = 512
TILES = BATCH * SEQ // P
SEQ_TILES = SEQ // P
ITS = BATCH * N_KV
STEPS = 2 * ITS
BLOCKS = STEP // QBLOCK
BANKS = BLOCKS // 2
MT = M_FFN // P
PAIRS = MT // 2
CH = 256
NF_CHUNKS = 3 * D // CH
NF_PER_STEP = NF_CHUNKS // 2
NF_ITS = MT

V_AT, K_AT, Q_AT = 0, KC * HD, 2 * KC * HD
QKV_COLS = Q_AT + KC * GROUP * HD
WO_COLS = GROUP * D

NF_LINES = [
    (0, 0.3038071990013123, -1.0),
    (7, 0.13015556335449219, 0.12570476531982422),
    (7, 0.09966795146465302, 0.014562472701072693),
    (7, 0.09105003625154495, 0.0),
    (8, 0.08134990185499191, 0.07958029955625534),
    (8, 0.09180293977260590, 0.06250641494989395),
    (8, 0.12190717458724976, -0.04691886901855469),
    (8, 0.27704316377639771, -0.93930214643478394),
]


def times(i, c, per, off):
    const = c * per + off
    assert const >= 0
    return const if i is None else i * (2 * per) + const


def build(nc, x, w_qkv, w_o, codes, absmax, out):
    ctx = ExitStack()
    with ctx:
        w_ffn = nc.dram_tensor("w_ffn_dram", (MT, P, 3 * D), F32).ap()
        sems = {}

        def sem(name):
            if name not in sems:
                sems[name] = ctx.enter_context(nc.semaphore(name))
            return sems[name]

        def sb(stack, name, shape, dt=F32):
            return stack.enter_context(nc.sbuf_tensor(name, shape, dt))

        resid = sb(ctx, "resid", [P, TILES, D])
        ident = sb(ctx, "ident", [P, P])
        stats = sb(ctx, "stats", [P, TILES, 6])
        meanvar = sb(ctx, "meanvar", [P, TILES, 2])
        std = sb(ctx, "std", [P, TILES])
        rstd = sb(ctx, "rstd", [P, TILES])
        eps = sb(ctx, "eps", [P, 1])

        with ExitStack() as att:
            xnT_hi = sb(att, "xnT_hi", [P, KC, SEQ], F32R)
            xnT_lo = sb(att, "xnT_lo", [P, KC, SEQ], F32R)
            qkv_hi = sb(att, "qkv_hi", [P, QKV_COLS], F32R)
            qkv_lo = sb(att, "qkv_lo", [P, QKV_COLS], F32R)
            wo_hi = sb(att, "wo_hi", [P, GROUP, D], F32R)
            wo_lo = sb(att, "wo_lo", [P, GROUP, D], F32R)
            w_raw = sb(att, "w_raw", [P, QKV_COLS])
            qT_hi = sb(att, "qT_hi", [P, GROUP // 2, BLOCKS, 2, QBLOCK], F32R)
            qT_lo = sb(att, "qT_lo", [P, GROUP // 2, BLOCKS, 2, QBLOCK], F32R)
            kT_hi = sb(att, "kT_hi", [P, 2, WINDOW + STEP], F32R)
            kT_lo = sb(att, "kT_lo", [P, 2, WINDOW + STEP], F32R)
            vT = sb(att, "vT", [P, 2, WINDOW + STEP])
            vwin_hi = sb(att, "vwin_hi", [P, BLOCKS, HD], F32R)
            vwin_lo = sb(att, "vwin_lo", [P, BLOCKS, HD], F32R)
            masked_s = sb(att, "masked_s", [P, 2, 4, P])
            probs = sb(att, "probs", [P, 2, 4, P])
            pT_hi = sb(att, "pT_hi", [P, 2, 2, 2 * P], F32R)
            pT_lo = sb(att, "pT_lo", [P, 2, 2, 2 * P], F32R)
            oT_hi = sb(att, "oT_hi", [P, GROUP, STEP], F32R)
            oT_lo = sb(att, "oT_lo", [P, GROUP, STEP], F32R)
            mask = sb(att, "mask", [P, 3, P])
            rowmax = sb(att, "rowmax", [P, 2, 4])
            negmax = sb(att, "negmax", [P, 2, 4])
            rowsum = sb(att, "rowsum", [P, 2, 4])
            rsum = sb(att, "rsum", [P, 2, 4])
            nf_q = sb(att, "nf_q", [P, 2, CH], I32)
            nf_am = sb(att, "nf_am", [P, 2, CH])
            nf_t7 = sb(att, "nf_t7", [P, CH])
            nf_t8 = sb(att, "nf_t8", [P, CH])
            nf_line = sb(att, "nf_line", [P, 8, CH])
            nf_w = sb(att, "nf_w", [P, 2, CH])
        with ExitStack() as ffn:
            x2T_hi = sb(ffn, "x2T_hi", [P, KC, TILES * P], F32R)
            x2T_lo = sb(ffn, "x2T_lo", [P, KC, TILES * P], F32R)
            wf_hi = sb(ffn, "wf_hi", [P, 2, 3, D], F32R)
            wf_lo = sb(ffn, "wf_lo", [P, 2, 3, D], F32R)
            wf_raw = sb(ffn, "wf_raw", [P, 2, 3, D])
            hT_hi = sb(ffn, "hT_hi", [P, 2, TILES * P], F32R)
            hT_lo = sb(ffn, "hT_lo", [P, 2, TILES * P], F32R)
            silu_g = sb(ffn, "silu_g", [P, 2, STEP])
            h_full = sb(ffn, "h_full", [P, 2, STEP])
            xn2 = sb(ffn, "xn2", [P, 2, D])

        def bank_pair(name):
            return [ctx.enter_context(nc.psum_tensor(f"{name}{k}", [P, STEP], F32)) for k in range(2)]

        ps_r, ps_s, ps_p, ps_o = (bank_pair(n) for n in ("ps_r", "ps_s", "ps_p", "ps_o"))

        def o_slot(oT, j):
            return oT[:, :, 2 * QBLOCK * j:2 * QBLOCK * (j + 1)].rearrange("p h (b q) -> p b h q", b=2)

        def o_psum(j):
            return ps_o[j % 2][:].rearrange("p (b h q) -> p b h q", b=2, h=GROUP)

        block = ctx.enter_context(nc.Block())

        @block.sync
        def _(sp):
            def load_x(c):
                sp.dma_start(resid[:, 4 * c:4 * c + 4, :],
                             x[4 * P * c:4 * P * (c + 1), :].rearrange("(t p) d -> p t d", p=P)
                             ).then_inc(sem(f"x_loaded{c}"), 16)

            def load_qkv(i, it, g):
                if i is not None or it:
                    sp.wait_ge(sem("wo_split"), times(i, 2 * it, 2, 0))
                sp.dma_start(w_raw[:], w_qkv[g]).then_inc(sem("raw_loaded"), 16)

            def load_wo(i, it, g):
                sp.wait_ge(sem("qkv_split"), times(i, 2 * it, 3, 6))
                sp.dma_start(w_raw[:, 0:WO_COLS], w_o[g]).then_inc(sem("raw_loaded"), 16)

            def nf_place(i, it, m):
                col = m * CH
                return (bass.ds(it if i is None else i + it, 1), slice(col, col + CH))

            def nf_load(i, it, m):
                tile, cols = nf_place(i, it, m)
                if i is not None or it or m >= 2:
                    sp.wait_ge(sem("nf_lines_done"), times(i, 2 * it, NF_PER_STEP, m - 1))
                    sp.wait_ge(sem("nf_dequantised"), times(i, 2 * it, NF_PER_STEP, m - 1))
                loaded = sem(f"nf_loaded{m % 2}")
                sp.dma_start(nf_q[:, m % 2, :], codes[tile, :, cols].rearrange("o p c -> (o p) c")
                             ).then_inc(loaded, 16)
                for half in range(2):
                    sp.dma_start(nf_am[64 * half:64 * half + 64, m % 2, :],
                                 absmax[tile, half, cols].broadcast_to([64, CH])).then_inc(loaded, 16)

            def nf_store(i, it, m):
                tile, cols = nf_place(i, it, m)
                sp.wait_ge(sem("nf_dequantised"), times(i, 2 * it, NF_PER_STEP, m + 1))
                sp.dma_start(w_ffn[tile, :, cols].rearrange("o p c -> (o p) c"),
                             nf_w[:, m % 2, :]).then_inc(sem(f"nf_stored{m % 2}"), 16)

            def iteration(i, it, g, next_g, nf):
                load_wo(i, it, g)
                for m in range(NF_CHUNKS) if nf else ():
                    nf_load(i, it, m)
                    if m:
                        nf_store(i, it, m - 1)
                    elif i is not None or it:
                        nf_store(i, it - 1, NF_CHUNKS - 1)
                    if m == NF_PER_STEP and next_g is not None:
                        load_qkv(i, it + 1, next_g)
                if not nf and next_g is not None:
                    load_qkv(i, it + 1, next_g)

            load_x(0)
            load_qkv(None, 0, 0)
            for c in range(1, TILES // 4):
                load_x(c)
            iteration(None, 0, 0, 1, True)
            with sp.Fori(0, N_KV - 2) as i:
                iteration(i, 1, group(i, 1), group(i, 2), True)
            iteration(None, N_KV - 1, N_KV - 1, 0, True)
            with sp.Fori(0, NF_ITS - N_KV) as i:
                iteration(i, N_KV, group(i, 0), group(i, 1), True)
            nf_store(None, NF_ITS - 1, NF_CHUNKS - 1)
            iteration(None, NF_ITS, NF_ITS - N_KV, NF_ITS - N_KV + 1, False)
            iteration(None, NF_ITS + 1, N_KV - 1, None, False)

            for k in range(2):
                sp.wait_ge(sem(f"nf_stored{k}"), 16 * MT * NF_CHUNKS // 2)
            sp.wait_ge(sem("out_added"), 4 * STEPS)
            for i in range(PAIRS):
                if i:
                    sp.wait_ge(sem("gateup_split"), i * 4)
                    sp.wait_ge(sem("down_split"), i * 2)
                sp.dma_start(wf_raw[:], w_ffn[2 * i:2 * i + 2].rearrange(
                    "t p (m d) -> p t m d", m=3)).then_inc(sem("wf_loaded"), 16)
            for t in range(TILES):
                sp.wait_ge(sem("down_added"), TILES * (PAIRS - 1) + t + 1)
                sp.dma_start(out[t * P:(t + 1) * P, :], resid[:, t, :]).then_inc(sem("stored"), 16)
            sp.wait_ge(sem("stored"), 16 * TILES)

        @block.gpsimd
        def _(pool):
            pool.memset(ident[:], 0.0).then_inc(sem("ident_zero"), 1)
            pool.wait_ge(sem("ident_zero"), 1)
            pool.affine_select(out=ident[:], in_=ident[:], compare_op=ALU.not_equal, fill=1.0, base=0,
                               pattern=[[-1, P]], channel_multiplier=1).then_inc(sem("ident_ready"), 1)
            pool.memset(mask[:], 0.0).then_inc(sem("mask_zero"), 1)
            pool.memset(kT_hi[:, 0, 0:WINDOW].bitcast(F32), 0.0)
            pool.memset(kT_lo[:, 0, 0:WINDOW].bitcast(F32), 0.0)
            pool.memset(vT[:, 0, 0:WINDOW], 0.0).then_inc(sem("pad_zero"), 1)
            pool.wait_ge(sem("mask_zero"), 1)
            pool.wait_ge(sem("pad_zero"), 1)
            for h in range(2):
                m = mask[64 * h:64 * h + 64, :, :]
                pool.affine_select(out=m, in_=m, compare_op=ALU.is_ge, fill=MASKED, base=-1,
                                   pattern=[[0, 3], [1, P]], channel_multiplier=-1
                                   ).then_inc(sem("mask_low"), 1)
                pool.wait_ge(sem("mask_low"), h + 1)
            for h in range(2):
                m = mask[64 * h:64 * h + 64, :, :]
                pool.affine_select(out=m, in_=m, compare_op=ALU.is_ge, fill=MASKED, base=WINDOW,
                                   pattern=[[0, 3], [-1, P]], channel_multiplier=1
                                   ).then_inc(sem("mask_high"), 1)
                pool.wait_ge(sem("mask_high"), h + 1)
            pool.memset(mask[:, 0, 0:WINDOW], MASKED).then_inc(sem("mask_ready"), 1)

            def waits_end():
                pool.sem_inc(sem("pool_waits"), 1)

            def split_qkv(i, it, at, to):
                last = QKV_COLS // 512
                if at == 0:
                    pool.wait_ge(sem("raw_loaded"), times(i, 2 * it, 16, 16))
                    if i is not None or it > 0:
                        pool.wait_ge(sem("proj_ready"), times(i, 2 * it, 6, 0))
                for k in range(at, to):
                    cols = slice(512 * k, 512 * k + 512)
                    if k == at:
                        waits_end()
                    pool.tensor_scalar(qkv_hi[:, cols], w_raw[:, cols], 1.0, 0.0, ALU.mult, ALU.add
                                       ).then_inc(sem("qkv_rounded"), 1)
                    pool.wait_ge(sem("qkv_rounded"), times(i, 2 * it, last // 2, k + 1))
                    pool.tensor_tensor(qkv_lo[:, cols], w_raw[:, cols], qkv_hi[:, cols].bitcast(F32),
                                       ALU.subtract).then_inc(sem("qkv_split"), 1)

            def split_wo(i, it):
                pool.wait_ge(sem("raw_loaded"), times(i, 2 * it, 16, 32))
                if i is not None or it > 0:
                    pool.wait_ge(sem("out_ready"), times(i, 2 * it, 4, 0))
                waits_end()
                for k in range(GROUP):
                    raw = w_raw[:, D * k:D * k + D]
                    pool.tensor_scalar(wo_hi[:, k, :], raw, 1.0, 0.0, ALU.mult, ALU.add
                                       ).then_inc(sem("wo_rounded"), 1)
                    pool.wait_ge(sem("wo_rounded"), times(i, 2 * it, GROUP // 2, k + 1))
                    pool.tensor_tensor(wo_lo[:, k, :], raw, wo_hi[:, k, :].bitcast(F32),
                                       ALU.subtract).then_inc(sem("wo_split"), 1)

            def nf_lines(i, it, m):
                q = nf_q[:, m % 2, :]
                pool.wait_ge(sem(f"nf_loaded{m % 2}"), times(i, 2 * it, 72, 48 * (m // 2 + 1)))
                if i is not None or it or m:
                    pool.wait_ge(sem("nf_dequantised"), times(i, 2 * it, NF_PER_STEP, m))
                waits_end()
                pool.tensor_scalar(nf_t7[:], q, 1.0, -7.0, ALU.mult, ALU.add).then_inc(sem("nf_shifted"), 1)
                pool.tensor_scalar(nf_t8[:], q, 1.0, -8.0, ALU.mult, ALU.add).then_inc(sem("nf_shifted"), 1)
                pool.wait_ge(sem("nf_shifted"), times(i, 2 * it, NF_CHUNKS, 2 * (m + 1)))
                waits_end()
                for j, (shift, slope, intercept) in enumerate(NF_LINES):
                    src = {0: q, 7: nf_t7[:], 8: nf_t8[:]}[shift]
                    last = pool.tensor_scalar(nf_line[:, j, :], src, slope, intercept, ALU.mult, ALU.add)
                last.then_inc(sem("nf_lines_done"), 1)

            def normalise(i, c, j):
                pool.wait_ge(sem("rsum_ready"), times(i, c, 4, j + 1))
                p = probs[:, j % 2]
                pool.tensor_tensor(p, p, rsum[:, j % 2, :, None].broadcast_to([P, 4, P]),
                                   ALU.mult).then_inc(sem("normalised"), 1)

            def iteration(i, it, nf, last=False):
                c = 2 * it
                for m in range(NF_PER_STEP) if nf else ():
                    nf_lines(i, it, m)
                for j in range(BANKS):
                    normalise(i, c, j)
                split_wo(i, it)
                for m in range(NF_PER_STEP, NF_CHUNKS) if nf else ():
                    nf_lines(i, it, m)
                for j in range(BANKS):
                    normalise(i, c + 1, j)
                    if not last and j < 3:
                        split_qkv(i, it + 1, 2 * j, 2 * j + 2)

            split_qkv(None, 0, 0, QKV_COLS // 512)
            iteration(None, 0, True)
            with pool.Fori(0, NF_ITS - 1) as i:
                iteration(i, 1, True)
            iteration(None, NF_ITS, False)
            iteration(None, NF_ITS + 1, False, last=True)

            pool.wait_ge(sem("out_added"), 4 * STEPS)

            def split_wf(i, off, kinds, name):
                n = 2 * len(kinds)
                waits_end()
                for a, (t, m) in enumerate((t, m) for t in range(2) for m in kinds):
                    raw = wf_raw[:, t, m, :]
                    pool.tensor_scalar(wf_hi[:, t, m, :], raw, 1.0, 0.0, ALU.mult, ALU.add
                                       ).then_inc(sem(name + "_rounded"), 1)
                    pool.wait_ge(sem(name + "_rounded"), (off * n + a + 1) if i is None else i * n + (off * n + a + 1))
                    pool.tensor_tensor(wf_lo[:, t, m, :], raw, wf_hi[:, t, m, :].bitcast(F32),
                                       ALU.subtract).then_inc(sem(name + "_split"), 1)

            def wf_down(i, off):
                split_wf(i, off, (2,), "down")

            def round_h(i, off):
                for n in range(8):
                    tb, t = n // 2, n % 2
                    pool.wait_ge(sem("h_ready"), (8 * off + n + 1) if i is None else i * 8 + (8 * off + n + 1))
                    if i is not None or off:
                        pool.wait_ge(sem("down_ready"), TILES * off if i is None else i * TILES + TILES * off)
                    waits_end()
                    pool.tensor_scalar(hT_hi[:, t, STEP * tb:STEP * tb + STEP], h_full[:, t, :],
                                       1.0, None, ALU.mult).then_inc(sem("h_rounded"), 1)

            pool.wait_ge(sem("wf_loaded"), 16)
            split_wf(None, 0, (0, 1), "gateup")
            wf_down(None, 0)
            with pool.Fori(0, PAIRS - 1) as i:
                round_h(i, 0)
                pool.wait_ge(sem("wf_loaded"), i * 16 + 32)
                pool.wait_ge(sem("up_ready"), i * 8 + 8)
                split_wf(i, 1, (0, 1), "gateup")
                pool.wait_ge(sem("down_ready"), i * TILES + TILES)
                wf_down(i, 1)
            round_h(None, PAIRS - 1)

        @block.scalar
        def _(act):
            def copy(out_, in_):
                return act.activation(out_, in_, ACT.Copy)

            def stds(t0, t1, n):
                act.wait_ge(sem("var_ready"), n)
                act.wait_ge(sem("eps_ready"), 1)
                act.activation(std[:, t0:t1], meanvar[:, t0:t1, 1], ACT.Sqrt, bias=eps[:, 0:1]
                               ).then_inc(sem("std_ready"), 1)

            def norm_hi(t, n, hi, at):
                act.wait_ge(sem("xnT_ready"), n + 1)
                copy(hi[:, :, at * P:at * P + P],
                     ps_r[n % 2][:].rearrange("p (k t) -> p k t", k=KC)).then_inc(sem("xnT_rounded"), 1)

            def step(i, c, first=False):
                u = c % 2
                act.wait_ge(sem("proj_ready"), times(i, c, 6, 1))
                if not first:
                    act.wait_ge(sem("vwin_ready"), times(i, c, 2, 0))
                else:
                    act.wait_ge(sem("pad_zero"), 1)
                ps = ps_r[0]
                if u == 0:
                    copy(vT[:, 1, 0:WINDOW], ps[:, STEP - WINDOW:STEP])
                copy(vT[:, u, WINDOW:], ps[:]).then_inc(sem("v_copied"), 1)
                act.wait_ge(sem("proj_ready"), times(i, c, 6, 2))
                if not first:
                    act.wait_ge(sem("score_ready"), times(i, c, 4, 0))
                ps = ps_r[1]
                if u == 0:
                    copy(kT_hi[:, 1, 0:WINDOW], ps[:, STEP - WINDOW:STEP])
                copy(kT_hi[:, u, WINDOW:], ps[:]).then_inc(sem("proj_rounded"), 1)
                for h in range(GROUP):
                    act.wait_ge(sem("proj_ready"), times(i, c, 6, 3 + h))
                    copy(qT_hi[:, h // 2, :, h % 2, :], ps_r[h % 2][:].rearrange("p (b q) -> p b q", b=BLOCKS)).then_inc(sem("proj_rounded"), 1)
                for k in range(2):
                    act.wait_ge(sem("vwin_ready"), times(i, c, 2, k + 1))
                    if not first:
                        act.wait_ge(sem("pv_ready"), times(i, c, 4, 0))
                    copy(vwin_hi[:, 4 * k:4 * k + 4, :], ps_r[k][:].rearrange("p (w d) -> p w d", w=4)
                         ).then_inc(sem("vwin_rounded"), 1)

                def exps(j):
                    act.wait_ge(sem("negmax_ready"), times(i, c, 4, j + 1))
                    if not first or j >= 2:
                        act.wait_ge(sem("pT_ready"), times(i, c, 4, j - 1))
                    for t in range(4):
                        last = act.activation(probs[:, j % 2, t, :], masked_s[:, j % 2, t, :], ACT.Exp,
                                              bias=negmax[:, j % 2, t:t + 1], scale=SCALE,
                                              accum_out=rowsum[:, j % 2, t:t + 1])
                    last.then_inc(sem("exp_done"), 1)

                def pT(j):
                    act.wait_ge(sem("pT_ready"), times(i, c, 4, j + 1))
                    if not first or j >= 2:
                        act.wait_ge(sem("pv_ready"), times(i, c, 4, j - 1))
                    copy(pT_hi[:, j % 2], ps_p[j % 2][:].rearrange("p (b q) -> p b q", b=2)
                         ).then_inc(sem("pT_rounded"), 1)

                def oT(j):
                    act.wait_ge(sem("pv_ready"), times(i, c, 4, j + 1))
                    if not first:
                        act.wait_ge(sem("out_ready"), times(i, c - 1, 4, j + 1))
                    copy(o_slot(oT_hi, j), o_psum(j)).then_inc(sem("oT_rounded"), 1)

                exps(0)
                exps(1)
                pT(0)
                exps(2)
                pT(1)
                exps(3)
                oT(0)
                pT(2)
                oT(1)
                pT(3)
                oT(2)
                oT(3)

            stds(0, SEQ_TILES, SEQ_TILES)
            for t in range(SEQ_TILES):
                norm_hi(t, t, xnT_hi, t)
            stds(SEQ_TILES, TILES, TILES)
            step(None, 0, True)
            step(None, 1)
            with act.Fori(0, N_KV - 1) as i:
                step(i, 2)
                step(i, 3)
            act.wait_ge(sem("proj_ready"), 6 * STEPS // 2)
            for t in range(SEQ_TILES, TILES):
                norm_hi(t, t, xnT_hi, t - SEQ_TILES)
            with act.Fori(0, N_KV) as i:
                step(i, 2 * N_KV)
                step(i, 2 * N_KV + 1)

            act.wait_ge(sem("out_added"), 4 * STEPS)
            for q in range(4):
                stds(4 * q, 4 * q + 4, TILES + 4 * q + 4)
                for t in range(4 * q, 4 * q + 4):
                    norm_hi(t, TILES + t, x2T_hi, t)
            with act.Fori(0, PAIRS) as i:
                for n in range(8):
                    act.wait_ge(sem("gate_ready"), i * 8 + (n + 1))
                    if n >= 2:
                        act.wait_ge(sem("h_ready"), i * 8 + (n - 1))
                    act.activation(silu_g[:, n % 2, :], ps_s[n % 2][:], ACT.Silu
                                   ).then_inc(sem("silu_ready"), 1)

        @block.vector
        def _(dve):
            def variances(t, n):
                dve.bn_stats(stats[:, t, :], resid[:, t, :]).then_inc(sem("stats_ready"), 1)
                dve.wait_ge(sem("stats_ready"), n + 1)
                dve.bn_aggr(meanvar[:, t, :], stats[:, t, :]).then_inc(sem("var_ready"), 1)

            def rstds(t0, t1, n):
                dve.wait_ge(sem("std_ready"), n)
                dve.reciprocal(rstd[:, t0:t1], std[:, t0:t1]).then_inc(sem("rstd_ready"), 1)

            def normalise(t, n, xn, r):
                dve.wait_ge(sem("rstd_ready"), r)
                if n >= 2:
                    dve.wait_ge(sem("xnT_ready"), n - 1)
                dve.tensor_scalar(xn, resid[:, t, :], meanvar[:, t, 0:1], rstd[:, t:t + 1],
                                  ALU.subtract, ALU.mult).then_inc(sem("xn_ready"), 1)

            def norm_lo(n, hi, lo, at):
                dve.wait_ge(sem("xnT_rounded"), n + 1)
                cols = slice(at * P, at * P + P)
                dve.tensor_tensor(lo[:, :, cols], ps_r[n % 2][:].rearrange("p (k t) -> p k t", k=KC),
                                  hi[:, :, cols].bitcast(F32), ALU.subtract
                                  ).then_inc(sem("xnT_split"), 1)

            def rest(lo, ps, hi):
                return dve.tensor_tensor(lo, ps, hi.bitcast(F32), ALU.subtract)

            def nf_combine(i, it, m):
                L = [nf_line[:, j, :] for j in range(8)]
                dve.wait_ge(sem("nf_lines_done"), times(i, 2 * it, NF_PER_STEP, m + 1))
                dve.scalar_tensor_tensor(L[0], L[0], 0.0, L[1], ALU.min, ALU.min)
                dve.tensor_tensor(L[2], L[2], L[3], ALU.min)
                dve.scalar_tensor_tensor(L[4], L[4], 0.0, L[5], ALU.max, ALU.max)
                dve.tensor_tensor(L[6], L[6], L[7], ALU.max).then_inc(sem("nf_quarters"), 1)
                dve.wait_ge(sem("nf_quarters"), times(i, 2 * it, NF_PER_STEP, m + 1))
                dve.tensor_tensor(L[1], L[0], L[2], ALU.min)
                dve.tensor_tensor(L[5], L[4], L[6], ALU.max).then_inc(sem("nf_halves"), 1)
                dve.wait_ge(sem("nf_halves"), times(i, 2 * it, NF_PER_STEP, m + 1))
                dve.tensor_tensor(L[3], L[1], L[5], ALU.add).then_inc(sem("nf_coded"), 1)
                if i is not None or it or m >= 2:
                    dve.wait_ge(sem(f"nf_stored{m % 2}"), times(i, 2 * it, 24, 16 * (m // 2)))
                dve.wait_ge(sem("nf_coded"), times(i, 2 * it, NF_PER_STEP, m + 1))
                dve.tensor_tensor(nf_w[:, m % 2, :], L[3], nf_am[:, m % 2, :], ALU.mult
                                  ).then_inc(sem("nf_dequantised"), 1)

            def step(i, c, nf, first=False):
                u = c % 2

                def keys():
                    dve.wait_ge(sem("proj_rounded"), times(i, c, 5, 1))
                    if u == 0:
                        rest(kT_lo[:, 1, 0:WINDOW], ps_r[1][:, STEP - WINDOW:STEP], kT_hi[:, 1, 0:WINDOW])
                    rest(kT_lo[:, u, WINDOW:], ps_r[1][:], kT_hi[:, u, WINDOW:]
                         ).then_inc(sem("proj_split"), 1)

                def queries(h):
                    dve.wait_ge(sem("proj_rounded"), times(i, c, 5, 2 + h))
                    rest(qT_lo[:, h // 2, :, h % 2, :], ps_r[h % 2][:].rearrange("p (b q) -> p b q", b=BLOCKS),
                         qT_hi[:, h // 2, :, h % 2, :]).then_inc(sem("proj_split"), 1)

                def vwin(k):
                    dve.wait_ge(sem("vwin_rounded"), times(i, c, 2, k + 1))
                    w = slice(4 * k, 4 * k + 4)
                    rest(vwin_lo[:, w, :], ps_r[k][:].rearrange("p (w d) -> p w d", w=4),
                         vwin_hi[:, w, :]).then_inc(sem("vwin_split"), 1)

                def softmax(j):
                    dve.wait_ge(sem("score_ready"), times(i, c, 4, j + 1))
                    if not first or j >= 2:
                        dve.wait_ge(sem("exp_done"), times(i, c, 4, j - 1))
                    m = 0 if u == 0 and j == 0 else 1
                    s = masked_s[:, j % 2]
                    dve.tensor_tensor(s.rearrange("p (b g) k -> p b g k", b=2),
                                      ps_s[j % 2][:].rearrange("p (b g k) -> p b g k", b=2, g=2),
                                      mask[:, m:m + 2, None, :].broadcast_to([P, 2, 2, P]),
                                      ALU.add).then_inc(sem("masked"), 1)
                    dve.wait_ge(sem("masked"), times(i, c, 4, j + 1))
                    dve.tensor_reduce(rowmax[:, j % 2, :], s, AX.X, ALU.max).then_inc(sem("max_ready"), 1)
                    dve.wait_ge(sem("max_ready"), times(i, c, 4, j + 1))
                    dve.tensor_scalar(negmax[:, j % 2, :], rowmax[:, j % 2, :], -SCALE, None, ALU.mult
                                      ).then_inc(sem("negmax_ready"), 1)

                def recip(j):
                    dve.wait_ge(sem("exp_done"), times(i, c, 4, j + 1))
                    if not first or j >= 2:
                        dve.wait_ge(sem("normalised"), times(i, c, 4, j - 1))
                    dve.reciprocal(rsum[:, j % 2, :], rowsum[:, j % 2, :]).then_inc(sem("rsum_ready"), 1)

                def pT(j):
                    dve.wait_ge(sem("pT_rounded"), times(i, c, 4, j + 1))
                    rest(pT_lo[:, j % 2], ps_p[j % 2][:].rearrange("p (b q) -> p b q", b=2), pT_hi[:, j % 2]
                         ).then_inc(sem("pT_split"), 1)

                def oT(j):
                    dve.wait_ge(sem("oT_rounded"), times(i, c, 4, j + 1))
                    rest(o_slot(oT_lo, j), o_psum(j), o_slot(oT_hi, j)).then_inc(sem("oT_split"), 1)

                def add_out(k):
                    if not first:
                        residual(i, c, k)

                def nf_part(k):
                    if nf:
                        nf_combine(i, c // 2, u * NF_PER_STEP + k)

                keys()
                queries(0)
                nf_part(0)
                queries(1)
                queries(2)
                nf_part(1)
                queries(3)
                vwin(0)
                vwin(1)
                softmax(0)
                nf_part(2)
                softmax(1)
                recip(0)
                softmax(2)
                recip(1)
                add_out(0)
                pT(0)
                softmax(3)
                recip(2)
                pT(1)
                add_out(1)
                recip(3)
                oT(0)
                pT(2)
                add_out(2)
                oT(1)
                pT(3)
                add_out(3)
                oT(2)
                oT(3)

            def residual(i, c, k):
                dve.wait_ge(sem("out_ready"), times(i, c - 1, 4, k + 1))
                u = (c - 1) % 2
                seq = 0 if c - 1 < STEPS // 2 else SEQ_TILES
                r = resid[:, seq + 4 * u + k, :]
                dve.tensor_tensor(r, ps_r[k % 2][:], r, ALU.add).then_inc(sem("out_added"), 1)

            dve.memset(eps[:], EPS).then_inc(sem("eps_ready"), 1)
            for t in range(SEQ_TILES):
                dve.wait_ge(sem(f"x_loaded{t // 4}"), 16)
                variances(t, t)
            rstds(0, SEQ_TILES, 1)
            for t in range(SEQ_TILES):
                normalise(t, t, masked_s[:, t % 2].rearrange("p a b -> p (a b)"), 1)
                if t:
                    norm_lo(t - 1, xnT_hi, xnT_lo, t - 1)
            norm_lo(SEQ_TILES - 1, xnT_hi, xnT_lo, SEQ_TILES - 1)
            for t in range(SEQ_TILES, TILES):
                dve.wait_ge(sem(f"x_loaded{t // 4}"), 16)
                variances(t, t)
            rstds(SEQ_TILES, TILES, 2)
            dve.wait_ge(sem("mask_ready"), 1)
            step(None, 0, True, first=True)
            step(None, 1, True)
            with dve.Fori(0, N_KV - 1) as i:
                step(i, 2, True)
                step(i, 3, True)
            dve.wait_ge(sem("exp_done"), 4 * STEPS // 2)
            for t in range(SEQ_TILES, TILES):
                normalise(t, t, masked_s[:, t % 2].rearrange("p a b -> p (a b)"), 2)
                if t > SEQ_TILES:
                    norm_lo(t - 1, xnT_hi, xnT_lo, t - 1 - SEQ_TILES)
            norm_lo(TILES - 1, xnT_hi, xnT_lo, SEQ_TILES - 1)
            step(None, 2 * N_KV, True)
            step(None, 2 * N_KV + 1, True)
            with dve.Fori(0, NF_ITS - N_KV - 1) as i:
                step(i, 2 * N_KV + 2, True)
                step(i, 2 * N_KV + 3, True)
            with dve.Fori(0, ITS - NF_ITS) as i:
                step(i, 2 * NF_ITS, False)
                step(i, 2 * NF_ITS + 1, False)
            for k in range(4):
                residual(None, STEPS, k)

            for q in range(4):
                for t in range(4 * q, 4 * q + 4):
                    dve.wait_ge(sem("out_added"), 4 * STEPS)
                    variances(t, TILES + t)
                rstds(4 * q, 4 * q + 4, 3 + q)
                for t in range(4 * q, 4 * q + 4):
                    normalise(t, TILES + t, xn2[:, t % 2, :], 3 + q)
                    if t:
                        norm_lo(TILES + t - 1, x2T_hi, x2T_lo, t - 1)
            norm_lo(2 * TILES - 1, x2T_hi, x2T_lo, TILES - 1)

            with dve.Fori(0, PAIRS) as i:
                def inner(n):
                    dve.wait_ge(sem("up_ready"), i * 8 + (n + 1))
                    dve.wait_ge(sem("silu_ready"), i * 8 + (n + 1))
                    if n >= 2:
                        dve.wait_ge(sem("h_split"), i * 8 + (n - 1))
                    dve.tensor_tensor(h_full[:, n % 2, :], ps_p[n % 2][:], silu_g[:, n % 2, :], ALU.mult
                                      ).then_inc(sem("h_ready"), 1)

                def inner_lo(n):
                    cols = slice(STEP * (n // 2), STEP * (n // 2) + STEP)
                    dve.wait_ge(sem("h_rounded"), i * 8 + (n + 1))
                    dve.tensor_tensor(hT_lo[:, n % 2, cols], h_full[:, n % 2, :],
                                      hT_hi[:, n % 2, cols].bitcast(F32), ALU.subtract
                                      ).then_inc(sem("h_split"), 1)

                for n in range(8):
                    inner(n)
                    if n:
                        inner_lo(n - 1)
                inner_lo(7)
                for t in range(TILES):
                    dve.wait_ge(sem("down_ready"), i * TILES + (t + 1))
                    r = resid[:, t, :]
                    dve.tensor_tensor(r, ps_o[t % 2][:], r, ALU.add).then_inc(sem("down_added"), 1)

        @block.tensor
        def _(pe):
            def product(ps, parts):
                n = 3 * len(parts)
                a = 0
                for (s_hi, s_lo), (m_hi, m_lo) in parts:
                    for s, m in ((s_hi, m_hi), (s_hi, m_lo), (s_lo, m_hi)):
                        last = pe.matmul(ps, s, m, start=(a == 0), stop=(a == n - 1))
                        a += 1
                return last

            def transposes(n, xn):
                pe.wait_ge(sem("xn_ready"), n + 1)
                if n >= 2:
                    pe.wait_ge(sem("xnT_split"), n - 1)
                for k in range(KC):
                    last = pe.transpose(ps_r[n % 2][:, k * P:k * P + P], xn[:, k * P:k * P + P], ident[:])
                last.then_inc(sem("xnT_ready"), 1)

            def step(i, c, first=False):
                u = c % 2
                toks = slice(STEP * u, STEP * u + STEP)

                def project(at, width, cols, bank):
                    def part(w, k):
                        a = at + k * width + cols
                        return w[:, a:a + HD]
                    return product(ps_r[bank][:], [
                        ((part(qkv_hi, k), part(qkv_lo, k)), (xnT_hi[:, k, toks], xnT_lo[:, k, toks]))
                        for k in range(KC)]).then_inc(sem("proj_ready"), 1)

                if u == 0:
                    pe.wait_ge(sem("qkv_split"), times(i, c, 3, 6))
                if first:
                    pe.wait_ge(sem("xnT_split"), SEQ_TILES)
                elif c == 1:
                    pe.wait_ge(sem("vwin_split"), 1)
                else:
                    pe.wait_ge(sem("out_added"), times(i, c - 2, 4, 3))
                project(V_AT, HD, 0, 0)
                if c == 1:
                    pe.wait_ge(sem("vwin_split"), 2)
                elif not first:
                    pe.wait_ge(sem("out_added"), times(i, c - 2, 4, 4))
                project(K_AT, HD, 0, 1)
                for h in range(GROUP):
                    if h == 0:
                        pe.wait_ge(sem("v_copied"), times(i, c, 1, 1))
                    else:
                        pe.wait_ge(sem("proj_split"), times(i, c, 5, h))
                    project(Q_AT, GROUP * HD, h * HD, h % 2)

                for k in range(2):
                    pe.wait_ge(sem("proj_split"), times(i, c, 5, 4 + k))
                    for w in range(4):
                        b = 4 * k + w
                        last = pe.transpose(ps_r[k][:, w * HD:w * HD + HD],
                                            vT[:, u, QBLOCK * b:QBLOCK * b + 2 * WINDOW], ident[:])
                    last.then_inc(sem("vwin_ready"), 1)

                def scores(j):
                    if not first or j >= 2:
                        pe.wait_ge(sem("masked"), times(i, c, 4, j - 1))
                    for b in range(2):
                        keys = slice(QBLOCK * (2 * j + b), QBLOCK * (2 * j + b) + 2 * WINDOW)
                        for g in range(2):
                            at = (2 * b + g) * P
                            last = product(ps_s[j % 2][:, at:at + P], [
                                (tuple(q[:, g, 2 * j + b].rearrange("p h q -> p (h q)") for q in (qT_hi, qT_lo)),
                                 (kT_hi[:, u, keys], kT_lo[:, u, keys]))])
                    last.then_inc(sem("score_ready"), 1)

                def probs_T(j):
                    pe.wait_ge(sem("normalised"), times(i, c, 4, j + 1))
                    if not first or j >= 2:
                        pe.wait_ge(sem("pT_split"), times(i, c, 4, j - 1))
                    for t in range(4):
                        last = pe.transpose(ps_p[j % 2][:, t * P:t * P + P], probs[:, j % 2, t, :], ident[:])
                    last.then_inc(sem("pT_ready"), 1)

                def values(j):
                    pe.wait_ge(sem("pT_split"), times(i, c, 4, j + 1))
                    pe.wait_ge(sem("vwin_split"), times(i, c, 2, j // 2 + 1))
                    if not first or j >= 2:
                        pe.wait_ge(sem("oT_split"), times(i, c, 4, j - 1))
                    for b in range(2):
                        last = product(ps_o[j % 2][:, b * 2 * P:(b + 1) * 2 * P], [
                            ((vwin_hi[:, 2 * j + b, :], vwin_lo[:, 2 * j + b, :]),
                             (pT_hi[:, j % 2, b, :], pT_lo[:, j % 2, b, :]))])
                    last.then_inc(sem("pv_ready"), 1)

                def out_tile(k):
                    if not first:
                        outputs(i, c, k)

                pe.wait_ge(sem("proj_split"), times(i, c, 5, 5))
                scores(0)
                scores(1)
                scores(2)
                out_tile(0)
                probs_T(0)
                scores(3)
                out_tile(1)
                probs_T(1)
                values(0)
                out_tile(2)
                probs_T(2)
                values(1)
                out_tile(3)
                probs_T(3)
                values(2)
                values(3)

            def outputs(i, c, k):
                pe.wait_ge(sem("oT_split"), times(i, c - 1, 4, k + 1))
                if k == 0:
                    pe.wait_ge(sem("wo_split"), times(i, (c - 1) // 2 * 2, 2, 4))
                if k < 2:
                    if c < STEPS:
                        pe.wait_ge(sem("vwin_split"), times(i, c, 2, k + 1))
                    else:
                        pe.wait_ge(sem("out_added"), times(i, c - 2, 4, 3 + k))
                else:
                    pe.wait_ge(sem("out_added"), times(i, c - 1, 4, k - 1))
                t = slice(k * P, k * P + P)
                product(ps_r[k % 2][:], [((oT_hi[:, h, t], oT_lo[:, h, t]), (wo_hi[:, h, :], wo_lo[:, h, :]))
                                         for h in range(GROUP)]).then_inc(sem("out_ready"), 1)

            pe.wait_ge(sem("ident_ready"), 1)
            for t in range(SEQ_TILES):
                transposes(t, masked_s[:, t % 2].rearrange("p a b -> p (a b)"))
            step(None, 0, True)
            step(None, 1)
            with pe.Fori(0, N_KV - 1) as i:
                step(i, 2)
                step(i, 3)
            pe.wait_ge(sem("out_added"), 4 * (STEPS // 2 - 1))
            for t in range(SEQ_TILES, TILES):
                transposes(t, masked_s[:, t % 2].rearrange("p a b -> p (a b)"))
            pe.wait_ge(sem("xnT_split"), TILES)
            with pe.Fori(0, N_KV) as i:
                step(i, 2 * N_KV)
                step(i, 2 * N_KV + 1)
            for k in range(4):
                outputs(None, STEPS, k)
            pe.wait_ge(sem("out_added"), 4 * STEPS)
            for t in range(TILES):
                transposes(TILES + t, xn2[:, t % 2, :])

            with pe.Fori(0, PAIRS) as i:
                pe.wait_ge(sem("gateup_split"), i * 4 + 4)
                for tb in range(4):
                    toks = slice(STEP * tb, STEP * tb + STEP)
                    pe.wait_ge(sem("xnT_split"), TILES + 4 * tb + 4)
                    for t in range(2):
                        n = 2 * tb + t
                        for m, ps, ready, free in ((0, ps_s, "gate_ready", "silu_ready"),
                                                   (1, ps_p, "up_ready", "h_ready")):
                            if n >= 2:
                                pe.wait_ge(sem(free), i * 8 + (n - 1))
                            product(ps[n % 2][:], [
                                ((wf_hi[:, t, m, k * P:k * P + P], wf_lo[:, t, m, k * P:k * P + P]),
                                 (x2T_hi[:, k, toks], x2T_lo[:, k, toks])) for k in range(KC)]
                                ).then_inc(sem(ready), 1)
                pe.wait_ge(sem("down_split"), i * 2 + 2)
                for t in range(TILES):
                    pe.wait_ge(sem("h_split"), i * 8 + 2 * (t // 4) + 2)
                    if t >= 2:
                        pe.wait_ge(sem("down_added"), i * TILES + (t - 1))
                    tt = slice(t * P, t * P + P)
                    product(ps_o[t % 2][:], [
                        ((hT_hi[:, a, tt], hT_lo[:, a, tt]), (wf_hi[:, a, 2, :], wf_lo[:, a, 2, :]))
                        for a in range(2)]).then_inc(sem("down_ready"), 1)


def group(i, off):
    return i + off


def kernel(**inputs):
    import concourse.bacc as bacc
    from concourse.bass_utils import run_bass_kernel_spmd

    def by_chunk(w, rows, cols):
        return w.reshape(rows // P, P, cols).transpose(1, 0, 2).reshape(P, -1)

    a = {k: np.asarray(v) for k, v in inputs.items()}
    wq, wk, wv, wo = (a[f"L0_attn_w{k}"] for k in "qkvo")
    gd = GROUP * HD
    w_qkv = np.stack([np.concatenate([by_chunk(wv[g * HD:(g + 1) * HD].T, D, HD),
                                      by_chunk(wk[g * HD:(g + 1) * HD].T, D, HD),
                                      by_chunk(wq[g * gd:(g + 1) * gd].T, D, gd)], 1) for g in range(N_KV)])
    w_o = np.stack([by_chunk(wo.T[g * gd:(g + 1) * gd], gd, D) for g in range(N_KV)])
    codes, scales = [], []
    gq, uq, dq = (a[f"L0_ffn_{k}_q"] for k in ("gate", "up", "down"))
    ga, ua = (a[f"L0_ffn_{k}_absmax"].reshape(M_FFN, D // 64) for k in ("gate", "up"))
    da = a["L0_ffn_down_absmax"].reshape(D, M_FFN // 64)
    for t in range(MT):
        m = slice(t * P, t * P + P)
        codes.append(np.concatenate([by_chunk(gq[m].T, D, P), by_chunk(uq[m].T, D, P), dq[:, m].T], 1))
        scales.append(np.concatenate([ga[m].T.reshape(KC, 2, P).transpose(1, 0, 2).reshape(2, -1),
                                      ua[m].T.reshape(KC, 2, P).transpose(1, 0, 2).reshape(2, -1),
                                      da[:, 2 * t:2 * t + 2].T], 1))
    arrays = {"x": a["L0_attn_x"].reshape(BATCH * SEQ, D), "w_qkv": w_qkv, "w_o": w_o,
              "codes": np.stack(codes), "absmax": np.stack(scales)}
    arrays = {f"{k}_dram": np.ascontiguousarray(v) for k, v in arrays.items()}

    nc = bacc.Bacc("TRN2", target_bir_lowering=False, num_devices=1)
    args = [nc.dram_tensor(k, v.shape, mybir.dt.from_np(v.dtype), kind="ExternalInput").ap()
            for k, v in arrays.items()]
    out = nc.dram_tensor("out_dram", (BATCH * SEQ, D), F32, kind="ExternalOutput").ap()
    build(nc, *args, out)
    r = run_bass_kernel_spmd(nc, [arrays], core_ids=[0])
    return r.results[0]["out_dram"].reshape(BATCH, SEQ, D)
```

```python
from contextlib import ExitStack

import concourse.bass as bass
import concourse.mybir as mybir
import numpy as np

F32 = mybir.dt.float32
F32R = mybir.dt.float32r
I32 = mybir.dt.int32
ALU = mybir.AluOpType
ACT = mybir.ActivationFunctionType
AX = mybir.AxisListType

P = 128
BATCH, SEQ, D = 2, 1024, 512
N_KV, GROUP, HD, WINDOW = 8, 4, 128, 64
M_FFN, QBLOCK = 1792, 64
EPS = 1e-5
SCALE = float(HD) ** -0.5
MASKED = -1.0e30

KC = D // P
STEP = 512
TILES = BATCH * SEQ // P
SEQ_TILES = SEQ // P
ITS = BATCH * N_KV
STEPS = 2 * ITS
BLOCKS = STEP // QBLOCK
BANKS = BLOCKS // 2
MT = M_FFN // P
PAIRS = MT // 2
CH = 256
NF_CHUNKS = 3 * D // CH
NF_PER_STEP = NF_CHUNKS // 2
NF_ITS = MT

V_AT, K_AT, Q_AT = 0, KC * HD, 2 * KC * HD
QKV_COLS = Q_AT + KC * GROUP * HD
WO_COLS = GROUP * D

NF_LINES = [
    (0, 0.3038071990013123, -1.0),
    (7, 0.13015556335449219, 0.12570476531982422),
    (7, 0.09966795146465302, 0.014562472701072693),
    (7, 0.09105003625154495, 0.0),
    (8, 0.08134990185499191, 0.07958029955625534),
    (8, 0.09180293977260590, 0.06250641494989395),
    (8, 0.12190717458724976, -0.04691886901855469),
    (8, 0.27704316377639771, -0.93930214643478394),
]


def times(i, c, per, off):
    const = c * per + off
    assert const >= 0
    return const if i is None else i * (2 * per) + const


def build(nc, x, w_qkv, w_o, codes, absmax, out):
    ctx = ExitStack()
    with ctx:
        w_ffn = nc.dram_tensor("w_ffn_dram", (MT, P, 3 * D), F32).ap()
        sems = {}

        def sem(name):
            if name not in sems:
                sems[name] = ctx.enter_context(nc.semaphore(name))
            return sems[name]

        def sb(stack, name, shape, dt=F32):
            return stack.enter_context(nc.sbuf_tensor(name, shape, dt))

        resid = sb(ctx, "resid", [P, TILES, D])
        ident = sb(ctx, "ident", [P, P])
        stats = sb(ctx, "stats", [P, TILES, 6])
        meanvar = sb(ctx, "meanvar", [P, TILES, 2])
        std = sb(ctx, "std", [P, TILES])
        rstd = sb(ctx, "rstd", [P, TILES])
        eps = sb(ctx, "eps", [P, 1])

        with ExitStack() as att:
            xnT_hi = sb(att, "xnT_hi", [P, KC, SEQ], F32R)
            xnT_lo = sb(att, "xnT_lo", [P, KC, SEQ], F32R)
            qkv_hi = sb(att, "qkv_hi", [P, QKV_COLS], F32R)
            qkv_lo = sb(att, "qkv_lo", [P, QKV_COLS], F32R)
            wo_hi = sb(att, "wo_hi", [P, GROUP, D], F32R)
            wo_lo = sb(att, "wo_lo", [P, GROUP, D], F32R)
            w_raw = sb(att, "w_raw", [P, QKV_COLS])
            qT = sb(att, "qT", [P, GROUP // 2, BLOCKS, 2, QBLOCK])
            kT = sb(att, "kT", [P, 2, WINDOW + STEP])
            vT = sb(att, "vT", [P, 2, WINDOW + STEP])
            vwin_hi = sb(att, "vwin_hi", [P, BLOCKS, HD], F32R)
            vwin_lo = sb(att, "vwin_lo", [P, BLOCKS, HD], F32R)
            masked_s = sb(att, "masked_s", [P, 2, 4, P])
            probs = sb(att, "probs", [P, 2, 4, P])
            pT_hi = sb(att, "pT_hi", [P, 2, 2, 2 * P], F32R)
            pT_lo = sb(att, "pT_lo", [P, 2, 2, 2 * P], F32R)
            oT_hi = sb(att, "oT_hi", [P, GROUP, STEP], F32R)
            oT_lo = sb(att, "oT_lo", [P, GROUP, STEP], F32R)
            mask = sb(att, "mask", [P, 2, P])
            rowmax = sb(att, "rowmax", [P, 2, 4])
            negmax = sb(att, "negmax", [P, 2, 4])
            rowsum = sb(att, "rowsum", [P, 2, 4])
            rsum = sb(att, "rsum", [P, 2, 4])
            nf_q = sb(att, "nf_q", [P, 2, CH], I32)
            nf_am = sb(att, "nf_am", [P, 2, CH])
            nf_line = sb(att, "nf_line", [P, 2, 8, CH])
        with ExitStack() as ffn:
            x2T_hi = sb(ffn, "x2T_hi", [P, KC, TILES * P], F32R)
            x2T_lo = sb(ffn, "x2T_lo", [P, KC, TILES * P], F32R)
            wf_hi = sb(ffn, "wf_hi", [P, 2, 3, D], F32R)
            wf_lo = sb(ffn, "wf_lo", [P, 2, 3, D], F32R)
            wf_raw = sb(ffn, "wf_raw", [P, 2, 3, D])
            hT_hi = sb(ffn, "hT_hi", [P, 2, TILES * P], F32R)
            hT_lo = sb(ffn, "hT_lo", [P, 2, TILES * P], F32R)
            silu_g = sb(ffn, "silu_g", [P, 2, STEP])
            h_full = sb(ffn, "h_full", [P, 2, STEP])
            xn2 = sb(ffn, "xn2", [P, 2, D])

        def bank_pair(name):
            return [ctx.enter_context(nc.psum_tensor(f"{name}{k}", [P, STEP], F32)) for k in range(2)]

        ps_r, ps_s, ps_p, ps_o = (bank_pair(n) for n in ("ps_r", "ps_s", "ps_p", "ps_o"))

        def o_slot(oT, j):
            return oT[:, :, 2 * QBLOCK * j:2 * QBLOCK * (j + 1)].rearrange("p h (b q) -> p b h q", b=2)

        def o_psum(j):
            return ps_o[j % 2][:].rearrange("p (b h q) -> p b h q", b=2, h=GROUP)

        block = ctx.enter_context(nc.Block())

        @block.sync
        def _(sp):
            def load_x(c):
                sp.dma_start(resid[:, 4 * c:4 * c + 4, :],
                             x[4 * P * c:4 * P * (c + 1), :].rearrange("(t p) d -> p t d", p=P)
                             ).then_inc(sem(f"x_loaded{c}"), 16)

            def load_qkv(i, it, g):
                if i is not None or it:
                    sp.wait_ge(sem("wo_split"), times(i, 2 * it, 2, 0))
                sp.dma_start(w_raw[:], w_qkv[g]).then_inc(sem("raw_loaded"), 16)

            def load_wo(i, it, g):
                sp.wait_ge(sem("qkv_split"), times(i, 2 * it, 3, 6))
                sp.dma_start(w_raw[:, 0:WO_COLS], w_o[g]).then_inc(sem("raw_loaded"), 16)

            def nf_place(i, it, m):
                col = m * CH
                return (bass.ds(it if i is None else i + it, 1), slice(col, col + CH))

            def nf_load(i, it, m):
                tile, cols = nf_place(i, it, m)
                if i is not None or it or m >= 2:
                    sp.wait_ge(sem("nf_lines_done"), times(i, 2 * it, NF_PER_STEP, m - 1))
                    sp.wait_ge(sem("nf_dequantised"), times(i, 2 * it, NF_PER_STEP, m - 1))
                loaded = sem(f"nf_loaded{m % 2}")
                sp.dma_start(nf_q[:, m % 2, :], codes[tile, :, cols].rearrange("o p c -> (o p) c")
                             ).then_inc(loaded, 16)
                for half in range(2):
                    sp.dma_start(nf_am[64 * half:64 * half + 64, m % 2, :],
                                 absmax[tile, half, cols].broadcast_to([64, CH])).then_inc(loaded, 16)

            def nf_store(i, it, m):
                tile, cols = nf_place(i, it, m)
                sp.wait_ge(sem("nf_dequantised"), times(i, 2 * it, NF_PER_STEP, m + 1))
                sp.dma_start(w_ffn[tile, :, cols].rearrange("o p c -> (o p) c"),
                             nf_line[:, m % 2, 0, :]).then_inc(sem(f"nf_stored{m % 2}"), 16)

            def iteration(i, it, g, next_g, nf):
                if nf:
                    nf_load(i, it, 0)
                    if i is not None or it:
                        nf_store(i, it - 1, NF_CHUNKS - 1)
                load_wo(i, it, g)
                for m in range(1, NF_CHUNKS) if nf else ():
                    nf_load(i, it, m)
                    if m == NF_CHUNKS - 1 and next_g is not None:
                        load_qkv(i, it + 1, next_g)
                    nf_store(i, it, m - 1)
                if not nf and next_g is not None:
                    load_qkv(i, it + 1, next_g)

            load_x(0)
            load_qkv(None, 0, 0)
            for c in range(1, TILES // 4):
                load_x(c)
            iteration(None, 0, 0, 1, True)
            with sp.Fori(0, N_KV - 2) as i:
                iteration(i, 1, group(i, 1), group(i, 2), True)
            iteration(None, N_KV - 1, N_KV - 1, 0, True)
            with sp.Fori(0, NF_ITS - N_KV) as i:
                iteration(i, N_KV, group(i, 0), group(i, 1), True)
            nf_store(None, NF_ITS - 1, NF_CHUNKS - 1)
            iteration(None, NF_ITS, NF_ITS - N_KV, NF_ITS - N_KV + 1, False)
            iteration(None, NF_ITS + 1, N_KV - 1, None, False)

            for k in range(2):
                sp.wait_ge(sem(f"nf_stored{k}"), 16 * MT * NF_CHUNKS // 2)
            sp.wait_ge(sem("out_added"), 4 * STEPS)
            for i in range(PAIRS):
                if i:
                    sp.wait_ge(sem("gateup_split"), i * 4)
                    sp.wait_ge(sem("down_split"), i * 2)
                sp.dma_start(wf_raw[:], w_ffn[2 * i:2 * i + 2].rearrange(
                    "t p (m d) -> p t m d", m=3)).then_inc(sem("wf_loaded"), 16)
            for t in range(TILES):
                sp.wait_ge(sem("down_added"), TILES * (PAIRS - 1) + t + 1)
                sp.dma_start(out[t * P:(t + 1) * P, :], resid[:, t, :]).then_inc(sem("stored"), 16)
            sp.wait_ge(sem("stored"), 16 * TILES)

        @block.gpsimd
        def _(pool):
            pool.memset(ident[:], 0.0).then_inc(sem("ident_zero"), 1)
            pool.wait_ge(sem("ident_zero"), 1)
            pool.affine_select(out=ident[:], in_=ident[:], compare_op=ALU.not_equal, fill=1.0, base=0,
                               pattern=[[-1, P]], channel_multiplier=1).then_inc(sem("ident_ready"), 1)
            pool.memset(mask[:], 0.0).then_inc(sem("mask_zero"), 1)
            pool.memset(kT[:, 0, 0:WINDOW], 0.0)
            pool.memset(vT[:, 0, 0:WINDOW], 0.0).then_inc(sem("pad_zero"), 1)
            pool.wait_ge(sem("mask_zero"), 1)
            pool.wait_ge(sem("pad_zero"), 1)
            for h in range(2):
                m = mask[64 * h:64 * h + 64, :, :]
                pool.affine_select(out=m, in_=m, compare_op=ALU.is_ge, fill=MASKED, base=-1,
                                   pattern=[[0, 2], [1, P]], channel_multiplier=-1
                                   ).then_inc(sem("mask_low"), 1)
                pool.wait_ge(sem("mask_low"), h + 1)
            for h in range(2):
                m = mask[64 * h:64 * h + 64, :, :]
                pool.affine_select(out=m, in_=m, compare_op=ALU.is_ge, fill=MASKED, base=WINDOW,
                                   pattern=[[0, 2], [-1, P]], channel_multiplier=1
                                   ).then_inc(sem("mask_high"), 1)
                pool.wait_ge(sem("mask_high"), h + 1)
            pool.memset(mask[:, 0, 0:WINDOW], MASKED).then_inc(sem("mask_ready"), 1)

            def waits_end():
                pool.sem_inc(sem("pool_waits"), 1)

            def split_qkv(i, it, at, to):
                last = QKV_COLS // 512
                if at == 0:
                    pool.wait_ge(sem("raw_loaded"), times(i, 2 * it, 16, 16))
                    if i is not None or it > 0:
                        pool.wait_ge(sem("proj_ready"), times(i, 2 * it, 6, 0))
                for k in range(at, to):
                    cols = slice(512 * k, 512 * k + 512)
                    if k == at:
                        waits_end()
                    pool.tensor_scalar(qkv_hi[:, cols], w_raw[:, cols], 1.0, 0.0, ALU.mult, ALU.add
                                       ).then_inc(sem("qkv_rounded"), 1)
                    pool.wait_ge(sem("qkv_rounded"), times(i, 2 * it, last // 2, k + 1))
                    pool.tensor_tensor(qkv_lo[:, cols], w_raw[:, cols], qkv_hi[:, cols].bitcast(F32),
                                       ALU.subtract).then_inc(sem("qkv_split"), 1)

            def split_wo(i, it):
                pool.wait_ge(sem("raw_loaded"), times(i, 2 * it, 16, 32))
                if i is not None or it > 0:
                    pool.wait_ge(sem("out_ready"), times(i, 2 * it, 4, 0))
                waits_end()
                for k in range(GROUP):
                    raw = w_raw[:, D * k:D * k + D]
                    pool.tensor_scalar(wo_hi[:, k, :], raw, 1.0, 0.0, ALU.mult, ALU.add
                                       ).then_inc(sem("wo_rounded"), 1)
                    pool.wait_ge(sem("wo_rounded"), times(i, 2 * it, GROUP // 2, k + 1))
                    pool.tensor_tensor(wo_lo[:, k, :], raw, wo_hi[:, k, :].bitcast(F32),
                                       ALU.subtract).then_inc(sem("wo_split"), 1)

            def nf_lines(i, it, m):
                q = nf_q[:, m % 2, :]
                pool.wait_ge(sem(f"nf_loaded{m % 2}"), times(i, 2 * it, 72, 48 * (m // 2 + 1)))
                if i is not None or it or m >= 2:
                    pool.wait_ge(sem(f"nf_stored{m % 2}"), times(i, 2 * it, 24, 16 * (m // 2)))
                waits_end()
                L = [nf_line[:, m % 2, j, :] for j in range(8)]
                pool.tensor_scalar(L[3], q, 1.0, -7.0, ALU.mult, ALU.add).then_inc(sem("nf_shifted"), 1)
                pool.tensor_scalar(L[7], q, 1.0, -8.0, ALU.mult, ALU.add).then_inc(sem("nf_shifted"), 1)
                pool.wait_ge(sem("nf_shifted"), times(i, 2 * it, NF_CHUNKS, 2 * (m + 1)))
                waits_end()
                for j in (0, 1, 2, 4, 5, 6):
                    shift, slope, intercept = NF_LINES[j]
                    last = pool.tensor_scalar(L[j], {0: q, 7: L[3], 8: L[7]}[shift], slope, intercept,
                                              ALU.mult, ALU.add)
                last.then_inc(sem("nf_six_lines"), 1)
                pool.wait_ge(sem("nf_six_lines"), times(i, 2 * it, NF_PER_STEP, m + 1))
                waits_end()
                for j in (3, 7):
                    _, slope, intercept = NF_LINES[j]
                    last = pool.tensor_scalar(L[j], L[j], slope, intercept, ALU.mult, ALU.add)
                last.then_inc(sem("nf_lines_done"), 1)

            def normalise(i, c, j):
                pool.wait_ge(sem("rsum_ready"), times(i, c, 4, j + 1))
                p = probs[:, j % 2]
                pool.tensor_tensor(p, p, rsum[:, j % 2, :, None].broadcast_to([P, 4, P]),
                                   ALU.mult).then_inc(sem("normalised"), 1)

            def iteration(i, it, nf, next_nf, last=False):
                c = 2 * it
                for m in range(1, NF_PER_STEP) if nf else ():
                    nf_lines(i, it, m)
                for j in range(BANKS):
                    normalise(i, c, j)
                if nf:
                    nf_lines(i, it, NF_PER_STEP)
                split_wo(i, it)
                for m in range(NF_PER_STEP + 1, NF_CHUNKS) if nf else ():
                    nf_lines(i, it, m)
                if not last:
                    split_qkv(i, it + 1, 0, 2)
                for j in range(BANKS):
                    normalise(i, c + 1, j)
                    if not last:
                        split_qkv(i, it + 1, j + 2, j + 3)
                if next_nf:
                    nf_lines(i, it + 1, 0)

            split_qkv(None, 0, 0, QKV_COLS // 512)
            nf_lines(None, 0, 0)
            iteration(None, 0, True, True)
            with pool.Fori(0, NF_ITS - 2) as i:
                iteration(i, 1, True, True)
            iteration(None, NF_ITS - 1, True, False)
            iteration(None, NF_ITS, False, False)
            iteration(None, NF_ITS + 1, False, False, last=True)

            pool.wait_ge(sem("out_added"), 4 * STEPS)

            def split_wf(i, off, kinds, name):
                n = 2 * len(kinds)
                waits_end()
                for a, (t, m) in enumerate((t, m) for t in range(2) for m in kinds):
                    raw = wf_raw[:, t, m, :]
                    pool.tensor_scalar(wf_hi[:, t, m, :], raw, 1.0, 0.0, ALU.mult, ALU.add
                                       ).then_inc(sem(name + "_rounded"), 1)
                    pool.wait_ge(sem(name + "_rounded"), (off * n + a + 1) if i is None else i * n + (off * n + a + 1))
                    pool.tensor_tensor(wf_lo[:, t, m, :], raw, wf_hi[:, t, m, :].bitcast(F32),
                                       ALU.subtract).then_inc(sem(name + "_split"), 1)

            def wf_down(i, off):
                split_wf(i, off, (2,), "down")

            def round_h(i, off):
                for n in range(8):
                    tb, t = n // 2, n % 2
                    pool.wait_ge(sem("h_ready"), (8 * off + n + 1) if i is None else i * 8 + (8 * off + n + 1))
                    waits_end()
                    pool.tensor_scalar(hT_hi[:, t, STEP * tb:STEP * tb + STEP], h_full[:, t, :],
                                       1.0, None, ALU.mult).then_inc(sem("h_rounded"), 1)

            pool.wait_ge(sem("wf_loaded"), 16)
            split_wf(None, 0, (0, 1), "gateup")
            wf_down(None, 0)
            with pool.Fori(0, PAIRS - 1) as i:
                round_h(i, 0)
                pool.wait_ge(sem("wf_loaded"), i * 16 + 32)
                pool.wait_ge(sem("up_ready"), i * 8 + 8)
                split_wf(i, 1, (0, 1), "gateup")
                pool.wait_ge(sem("down_ready"), i * TILES + TILES)
                wf_down(i, 1)
            round_h(None, PAIRS - 1)

        @block.scalar
        def _(act):
            def copy(out_, in_):
                return act.activation(out_, in_, ACT.Copy)

            def stds(t0, t1, n):
                act.wait_ge(sem("var_ready"), n)
                act.wait_ge(sem("eps_ready"), 1)
                act.activation(std[:, t0:t1], meanvar[:, t0:t1, 1], ACT.Sqrt, bias=eps[:, 0:1]
                               ).then_inc(sem("std_ready"), 1)

            def norm_hi(t, n, hi, at):
                act.wait_ge(sem("xnT_ready"), n + 1)
                copy(hi[:, :, at * P:at * P + P],
                     ps_r[n % 2][:].rearrange("p (k t) -> p k t", k=KC)).then_inc(sem("xnT_rounded"), 1)

            def step(i, c, first=False):
                u = c % 2
                act.wait_ge(sem("proj_ready"), times(i, c, 6, 1))
                if not first:
                    act.wait_ge(sem("vwin_ready"), times(i, c, 2, 0))
                else:
                    act.wait_ge(sem("pad_zero"), 1)
                ps = ps_r[0]
                if u == 0:
                    copy(vT[:, 1, 0:WINDOW], ps[:, STEP - WINDOW:STEP])
                copy(vT[:, u, WINDOW:], ps[:]).then_inc(sem("v_copied"), 1)
                act.wait_ge(sem("proj_ready"), times(i, c, 6, 2))
                if not first:
                    act.wait_ge(sem("score_ready"), times(i, c, 4, 0))
                ps = ps_r[1]
                if u == 0:
                    copy(kT[:, 1, 0:WINDOW], ps[:, STEP - WINDOW:STEP])
                copy(kT[:, u, WINDOW:], ps[:]).then_inc(sem("qk_copied"), 1)
                for h in range(GROUP):
                    act.wait_ge(sem("proj_ready"), times(i, c, 6, 3 + h))
                    copy(qT[:, h // 2, :, h % 2, :], ps_r[h % 2][:].rearrange(
                        "p (b q) -> p b q", b=BLOCKS)).then_inc(sem("qk_copied"), 1)
                    k = h
                    if k >= 2:
                        continue
                    act.wait_ge(sem("vwin_ready"), times(i, c, 2, k + 1))
                    if not first:
                        act.wait_ge(sem("pv_ready"), times(i, c, 4, 0))
                    copy(vwin_hi[:, 4 * k:4 * k + 4, :], ps_p[k][:].rearrange("p (w d) -> p w d", w=4)
                         ).then_inc(sem("vwin_rounded"), 1)

                def exps(j):
                    act.wait_ge(sem("negmax_ready"), times(i, c, 4, j + 1))
                    if not first or j >= 2:
                        act.wait_ge(sem("pT_ready"), times(i, c, 4, j - 1))
                    for t in range(4):
                        last = act.activation(probs[:, j % 2, t, :], masked_s[:, j % 2, t, :], ACT.Exp,
                                              bias=negmax[:, j % 2, t:t + 1], scale=SCALE,
                                              accum_out=rowsum[:, j % 2, t:t + 1])
                    last.then_inc(sem("exp_done"), 1)

                def pT(j):
                    act.wait_ge(sem("pT_ready"), times(i, c, 4, j + 1))
                    if not first or j >= 2:
                        act.wait_ge(sem("pv_ready"), times(i, c, 4, j - 1))
                    copy(pT_hi[:, j % 2], ps_p[j % 2][:].rearrange("p (b q) -> p b q", b=2)
                         ).then_inc(sem("pT_rounded"), 1)

                def oT(j):
                    act.wait_ge(sem("pv_ready"), times(i, c, 4, j + 1))
                    if not first:
                        act.wait_ge(sem("out_ready"), times(i, c - 1, 4, j + 1))
                    copy(o_slot(oT_hi, j), o_psum(j)).then_inc(sem("oT_rounded"), 1)

                exps(0)
                exps(1)
                pT(0)
                exps(2)
                pT(1)
                exps(3)
                oT(0)
                pT(2)
                oT(1)
                pT(3)
                oT(2)
                oT(3)

            stds(0, SEQ_TILES, SEQ_TILES)
            for t in range(SEQ_TILES):
                norm_hi(t, t, xnT_hi, t)
            stds(SEQ_TILES, TILES, TILES)
            step(None, 0, True)
            step(None, 1)
            with act.Fori(0, N_KV - 1) as i:
                step(i, 2)
                step(i, 3)
            act.wait_ge(sem("proj_ready"), 6 * STEPS // 2)
            for t in range(SEQ_TILES, TILES):
                norm_hi(t, t, xnT_hi, t - SEQ_TILES)
            with act.Fori(0, N_KV) as i:
                step(i, 2 * N_KV)
                step(i, 2 * N_KV + 1)

            act.wait_ge(sem("out_added"), 4 * STEPS)
            for q in range(4):
                stds(4 * q, 4 * q + 4, TILES + 4 * q + 4)
                for t in range(4 * q, 4 * q + 4):
                    norm_hi(t, TILES + t, x2T_hi, t)
            with act.Fori(0, PAIRS) as i:
                for n in range(8):
                    act.wait_ge(sem("gate_ready"), i * 8 + (n + 1))
                    if n >= 2:
                        act.wait_ge(sem("h_ready"), i * 8 + (n - 1))
                    act.activation(silu_g[:, n % 2, :], ps_s[n % 2][:], ACT.Silu
                                   ).then_inc(sem("silu_ready"), 1)

        @block.vector
        def _(dve):
            def variances(t, n):
                dve.bn_stats(stats[:, t, :], resid[:, t, :]).then_inc(sem("stats_ready"), 1)
                dve.wait_ge(sem("stats_ready"), n + 1)
                dve.bn_aggr(meanvar[:, t, :], stats[:, t, :]).then_inc(sem("var_ready"), 1)

            def rstds(t0, t1, n):
                dve.wait_ge(sem("std_ready"), n)
                dve.reciprocal(rstd[:, t0:t1], std[:, t0:t1]).then_inc(sem("rstd_ready"), 1)

            def normalise(t, n, xn, r):
                dve.wait_ge(sem("rstd_ready"), r)
                if n >= 2:
                    dve.wait_ge(sem("xnT_ready"), n - 1)
                dve.tensor_scalar(xn, resid[:, t, :], meanvar[:, t, 0:1], rstd[:, t:t + 1],
                                  ALU.subtract, ALU.mult).then_inc(sem("xn_ready"), 1)

            def norm_lo(n, hi, lo, at):
                dve.wait_ge(sem("xnT_rounded"), n + 1)
                cols = slice(at * P, at * P + P)
                dve.tensor_tensor(lo[:, :, cols], ps_r[n % 2][:].rearrange("p (k t) -> p k t", k=KC),
                                  hi[:, :, cols].bitcast(F32), ALU.subtract
                                  ).then_inc(sem("xnT_split"), 1)

            def rest(lo, ps, hi):
                return dve.tensor_tensor(lo, ps, hi.bitcast(F32), ALU.subtract)

            def nf_least(i, it, m):
                L = [nf_line[:, m % 2, j, :] for j in range(8)]
                dve.wait_ge(sem("nf_lines_done"), times(i, 2 * it, NF_PER_STEP, m + 1))
                dve.scalar_tensor_tensor(L[0], L[0], 0.0, L[1], ALU.min, ALU.min)
                dve.tensor_tensor(L[2], L[2], L[3], ALU.min)
                dve.scalar_tensor_tensor(L[4], L[4], 0.0, L[5], ALU.max, ALU.max)
                dve.tensor_tensor(L[6], L[6], L[7], ALU.max).then_inc(sem("nf_quarters"), 1)

            def nf_combine(i, it, m):
                L = [nf_line[:, m % 2, j, :] for j in range(8)]
                dve.wait_ge(sem("nf_quarters"), times(i, 2 * it, NF_PER_STEP, m + 1))
                dve.tensor_tensor(L[1], L[0], L[2], ALU.min)
                dve.tensor_tensor(L[5], L[4], L[6], ALU.max).then_inc(sem("nf_halves"), 1)
                dve.wait_ge(sem("nf_halves"), times(i, 2 * it, NF_PER_STEP, m + 1))
                dve.tensor_tensor(L[3], L[1], L[5], ALU.add).then_inc(sem("nf_coded"), 1)
                dve.wait_ge(sem("nf_coded"), times(i, 2 * it, NF_PER_STEP, m + 1))
                dve.tensor_tensor(L[0], L[3], nf_am[:, m % 2, :], ALU.mult
                                  ).then_inc(sem("nf_dequantised"), 1)

            def step(i, c, nf, first=False):
                u = c % 2

                def vwin(k):
                    dve.wait_ge(sem("vwin_rounded"), times(i, c, 2, k + 1))
                    w = slice(4 * k, 4 * k + 4)
                    rest(vwin_lo[:, w, :], ps_p[k][:].rearrange("p (w d) -> p w d", w=4),
                         vwin_hi[:, w, :]).then_inc(sem("vwin_split"), 1)

                def softmax(j):
                    dve.wait_ge(sem("score_ready"), times(i, c, 4, j + 1))
                    if not first or j >= 2:
                        dve.wait_ge(sem("exp_done"), times(i, c, 4, j - 1))
                    m = mask[:, 0:2] if u == 0 and j == 0 else mask[:, 1:2].broadcast_to([P, 2, P])
                    s = masked_s[:, j % 2]
                    dve.tensor_tensor(s.rearrange("p (b g) k -> p b g k", b=2),
                                      ps_s[j % 2][:].rearrange("p (b g k) -> p b g k", b=2, g=2),
                                      m[:, :, None, :].broadcast_to([P, 2, 2, P]),
                                      ALU.add).then_inc(sem("masked"), 1)
                    dve.wait_ge(sem("masked"), times(i, c, 4, j + 1))
                    dve.tensor_reduce(rowmax[:, j % 2, :], s, AX.X, ALU.max).then_inc(sem("max_ready"), 1)
                    dve.wait_ge(sem("max_ready"), times(i, c, 4, j + 1))
                    dve.tensor_scalar(negmax[:, j % 2, :], rowmax[:, j % 2, :], -SCALE, None, ALU.mult
                                      ).then_inc(sem("negmax_ready"), 1)

                def recip(j):
                    dve.wait_ge(sem("exp_done"), times(i, c, 4, j + 1))
                    if not first or j >= 2:
                        dve.wait_ge(sem("normalised"), times(i, c, 4, j - 1))
                    dve.reciprocal(rsum[:, j % 2, :], rowsum[:, j % 2, :]).then_inc(sem("rsum_ready"), 1)

                def pT(j):
                    dve.wait_ge(sem("pT_rounded"), times(i, c, 4, j + 1))
                    rest(pT_lo[:, j % 2], ps_p[j % 2][:].rearrange("p (b q) -> p b q", b=2), pT_hi[:, j % 2]
                         ).then_inc(sem("pT_split"), 1)

                def oT(j):
                    dve.wait_ge(sem("oT_rounded"), times(i, c, 4, j + 1))
                    rest(o_slot(oT_lo, j), o_psum(j), o_slot(oT_hi, j)).then_inc(sem("oT_split"), 1)

                def add_out(k):
                    if not first:
                        residual(i, c, k)

                def nf_part(k):
                    if nf:
                        (nf_combine if k % 2 else nf_least)(i, c // 2, u * NF_PER_STEP + k // 2)

                nf_part(0)
                nf_part(1)
                vwin(0)
                vwin(1)
                nf_part(2)
                nf_part(3)
                nf_part(4)
                softmax(0)
                softmax(1)
                add_out(0)
                recip(0)
                softmax(2)
                recip(1)
                softmax(3)
                add_out(1)
                pT(0)
                nf_part(5)
                recip(2)
                pT(1)
                add_out(2)
                recip(3)
                oT(0)
                pT(2)
                oT(1)
                add_out(3)
                pT(3)
                oT(2)
                oT(3)

            def residual(i, c, k):
                dve.wait_ge(sem("out_ready"), times(i, c - 1, 4, k + 1))
                u = (c - 1) % 2
                seq = 0 if c - 1 < STEPS // 2 else SEQ_TILES
                r = resid[:, seq + 4 * u + k, :]
                dve.tensor_tensor(r, ps_r[k % 2][:], r, ALU.add).then_inc(sem("out_added"), 1)

            dve.memset(eps[:], EPS).then_inc(sem("eps_ready"), 1)
            for t in range(SEQ_TILES):
                dve.wait_ge(sem(f"x_loaded{t // 4}"), 16)
                variances(t, t)
            rstds(0, SEQ_TILES, 1)
            for t in range(SEQ_TILES):
                normalise(t, t, masked_s[:, t % 2].rearrange("p a b -> p (a b)"), 1)
                if t:
                    norm_lo(t - 1, xnT_hi, xnT_lo, t - 1)
            norm_lo(SEQ_TILES - 1, xnT_hi, xnT_lo, SEQ_TILES - 1)
            for t in range(SEQ_TILES, TILES):
                dve.wait_ge(sem(f"x_loaded{t // 4}"), 16)
                variances(t, t)
            rstds(SEQ_TILES, TILES, 2)
            dve.wait_ge(sem("mask_ready"), 1)
            step(None, 0, True, first=True)
            step(None, 1, True)
            with dve.Fori(0, N_KV - 1) as i:
                step(i, 2, True)
                step(i, 3, True)
            dve.wait_ge(sem("exp_done"), 4 * STEPS // 2)
            for t in range(SEQ_TILES, TILES):
                normalise(t, t, masked_s[:, t % 2].rearrange("p a b -> p (a b)"), 2)
                if t > SEQ_TILES:
                    norm_lo(t - 1, xnT_hi, xnT_lo, t - 1 - SEQ_TILES)
            norm_lo(TILES - 1, xnT_hi, xnT_lo, SEQ_TILES - 1)
            step(None, 2 * N_KV, True)
            step(None, 2 * N_KV + 1, True)
            with dve.Fori(0, NF_ITS - N_KV - 1) as i:
                step(i, 2 * N_KV + 2, True)
                step(i, 2 * N_KV + 3, True)
            with dve.Fori(0, ITS - NF_ITS) as i:
                step(i, 2 * NF_ITS, False)
                step(i, 2 * NF_ITS + 1, False)
            for k in range(4):
                residual(None, STEPS, k)

            for q in range(4):
                for t in range(4 * q, 4 * q + 4):
                    dve.wait_ge(sem("out_added"), 4 * STEPS)
                    variances(t, TILES + t)
                rstds(4 * q, 4 * q + 4, 3 + q)
                for t in range(4 * q, 4 * q + 4):
                    normalise(t, TILES + t, xn2[:, t % 2, :], 3 + q)
                    if t:
                        norm_lo(TILES + t - 1, x2T_hi, x2T_lo, t - 1)
            norm_lo(2 * TILES - 1, x2T_hi, x2T_lo, TILES - 1)

            with dve.Fori(0, PAIRS) as i:
                def inner(n):
                    dve.wait_ge(sem("up_ready"), i * 8 + (n + 1))
                    dve.wait_ge(sem("silu_ready"), i * 8 + (n + 1))
                    if n >= 2:
                        dve.wait_ge(sem("h_split"), i * 8 + (n - 1))
                    dve.tensor_tensor(h_full[:, n % 2, :], ps_p[n % 2][:], silu_g[:, n % 2, :], ALU.mult
                                      ).then_inc(sem("h_ready"), 1)

                def inner_lo(n):
                    cols = slice(STEP * (n // 2), STEP * (n // 2) + STEP)
                    dve.wait_ge(sem("h_rounded"), i * 8 + (n + 1))
                    dve.tensor_tensor(hT_lo[:, n % 2, cols], h_full[:, n % 2, :],
                                      hT_hi[:, n % 2, cols].bitcast(F32), ALU.subtract
                                      ).then_inc(sem("h_split"), 1)

                for n in range(8):
                    inner(n)
                    if n:
                        inner_lo(n - 1)
                inner_lo(7)
                for t in range(TILES):
                    dve.wait_ge(sem("down_ready"), i * TILES + (t + 1))
                    r = resid[:, t, :]
                    dve.tensor_tensor(r, ps_o[t % 2][:], r, ALU.add).then_inc(sem("down_added"), 1)

        @block.tensor
        def _(pe):
            def product(ps, parts):
                n = 3 * len(parts)
                a = 0
                for (s_hi, s_lo), (m_hi, m_lo) in parts:
                    for s, m in ((s_hi, m_hi), (s_hi, m_lo), (s_lo, m_hi)):
                        last = pe.matmul(ps, s, m, start=(a == 0), stop=(a == n - 1))
                        a += 1
                return last

            def transposes(n, xn):
                pe.wait_ge(sem("xn_ready"), n + 1)
                if n >= 2:
                    pe.wait_ge(sem("xnT_split"), n - 1)
                for k in range(KC):
                    last = pe.transpose(ps_r[n % 2][:, k * P:k * P + P], xn[:, k * P:k * P + P], ident[:])
                last.then_inc(sem("xnT_ready"), 1)

            def project(i, c, at, width, cols, bank):
                toks = slice(STEP * (c % 2), STEP * (c % 2) + STEP)

                def part(w, k):
                    a = at + k * width + cols
                    return w[:, a:a + HD]
                product(ps_r[bank][:], [
                    ((part(qkv_hi, k), part(qkv_lo, k)), (xnT_hi[:, k, toks], xnT_lo[:, k, toks]))
                    for k in range(KC)]).then_inc(sem("proj_ready"), 1)

            def values_of(i, c):
                if c % 2 == 0:
                    pe.wait_ge(sem("qkv_split"), times(i, c, 3, 1))
                if i is not None or c >= 2:
                    pe.wait_ge(sem("out_added"), times(i, c - 2, 4, 3))
                project(i, c, V_AT, HD, 0, 0)

            def keys_of(i, c):
                if i is not None or c >= 2:
                    pe.wait_ge(sem("out_added"), times(i, c - 2, 4, 4))
                if c % 2 == 0:
                    pe.wait_ge(sem("qkv_split"), times(i, c, 3, 2))
                project(i, c, K_AT, HD, 0, 1)

            def step(i, c, first=False, ahead=True):
                u = c % 2

                def windows(k):
                    if not first:
                        pe.wait_ge(sem("pT_split"), times(i, c, 4, k - 1))
                    for w in range(4):
                        b = 4 * k + w
                        last = pe.transpose(ps_p[k][:, w * HD:w * HD + HD],
                                            vT[:, u, QBLOCK * b:QBLOCK * b + 2 * WINDOW], ident[:])
                    last.then_inc(sem("vwin_ready"), 1)

                for h in range(GROUP):
                    if h == 0:
                        pe.wait_ge(sem("v_copied"), times(i, c, 1, 1))
                        if u == 0:
                            pe.wait_ge(sem("qkv_split"), times(i, c, 3, 6))
                    else:
                        pe.wait_ge(sem("qk_copied"), times(i, c, 5, h))
                    project(i, c, Q_AT, GROUP * HD, h * HD, h % 2)
                    if h < 2:
                        windows(h)

                def scores(j, g):
                    if g == 0 and (not first or j >= 2):
                        pe.wait_ge(sem("masked"), times(i, c, 4, j - 1))
                    for b in range(2):
                        keys = slice(QBLOCK * (2 * j + b), QBLOCK * (2 * j + b) + 2 * WINDOW)
                        at = (2 * b + g) * P
                        last = pe.matmul(ps_s[j % 2][:, at:at + P],
                                         qT[:, g, 2 * j + b].rearrange("p h q -> p (h q)"),
                                         kT[:, u, keys], start=True, stop=True)
                    if g == 1:
                        last.then_inc(sem("score_ready"), 1)

                def probs_T(j):
                    pe.wait_ge(sem("normalised"), times(i, c, 4, j + 1))
                    if j >= 2:
                        pe.wait_ge(sem("pT_split"), times(i, c, 4, j - 1))
                    else:
                        pe.wait_ge(sem("vwin_split"), times(i, c, 2, j + 1))
                    for t in range(4):
                        last = pe.transpose(ps_p[j % 2][:, t * P:t * P + P], probs[:, j % 2, t, :], ident[:])
                    last.then_inc(sem("pT_ready"), 1)

                def values(j):
                    pe.wait_ge(sem("pT_split"), times(i, c, 4, j + 1))
                    pe.wait_ge(sem("vwin_split"), times(i, c, 2, j // 2 + 1))
                    if not first or j >= 2:
                        pe.wait_ge(sem("oT_split"), times(i, c, 4, j - 1))
                    for b in range(2):
                        last = product(ps_o[j % 2][:, b * 2 * P:(b + 1) * 2 * P], [
                            ((vwin_hi[:, 2 * j + b, :], vwin_lo[:, 2 * j + b, :]),
                             (pT_hi[:, j % 2, b, :], pT_lo[:, j % 2, b, :]))])
                    last.then_inc(sem("pv_ready"), 1)

                def out_tile(k):
                    if not first:
                        outputs(i, c, k)

                pe.wait_ge(sem("qk_copied"), times(i, c, 5, 3))
                scores(0, 0)
                scores(1, 0)
                pe.wait_ge(sem("qk_copied"), times(i, c, 5, 5))
                scores(0, 1)
                scores(1, 1)
                out_tile(0)
                scores(2, 0)
                scores(2, 1)
                scores(3, 0)
                scores(3, 1)
                out_tile(1)
                probs_T(0)
                probs_T(1)
                out_tile(2)
                values(0)
                probs_T(2)
                values(1)
                out_tile(3)
                probs_T(3)
                values(2)
                if ahead:
                    values_of(i, c + 1)
                values(3)
                if ahead:
                    keys_of(i, c + 1)

            def outputs(i, c, k):
                pe.wait_ge(sem("oT_split"), times(i, c - 1, 4, k + 1))
                if k == 0:
                    pe.wait_ge(sem("wo_split"), times(i, (c - 1) // 2 * 2, 2, 4))
                if k < 2:
                    if c < STEPS:
                        pe.wait_ge(sem("qk_copied"), times(i, c, 5, 4 + k))
                    else:
                        pe.wait_ge(sem("out_added"), times(i, c - 2, 4, 3 + k))
                else:
                    pe.wait_ge(sem("out_added"), times(i, c - 1, 4, k - 1))
                t = slice(k * P, k * P + P)
                product(ps_r[k % 2][:], [((oT_hi[:, h, t], oT_lo[:, h, t]), (wo_hi[:, h, :], wo_lo[:, h, :]))
                                         for h in range(GROUP)]).then_inc(sem("out_ready"), 1)

            pe.wait_ge(sem("ident_ready"), 1)
            for t in range(SEQ_TILES):
                transposes(t, masked_s[:, t % 2].rearrange("p a b -> p (a b)"))
            pe.wait_ge(sem("xnT_split"), SEQ_TILES)
            values_of(None, 0)
            keys_of(None, 0)
            step(None, 0, True)
            step(None, 1)
            with pe.Fori(0, N_KV - 2) as i:
                step(i, 2)
                step(i, 3)
            step(None, 2 * N_KV - 2)
            step(None, 2 * N_KV - 1, ahead=False)
            pe.wait_ge(sem("out_added"), 4 * (STEPS // 2 - 1))
            for t in range(SEQ_TILES, TILES):
                transposes(t, masked_s[:, t % 2].rearrange("p a b -> p (a b)"))
            pe.wait_ge(sem("xnT_split"), TILES)
            values_of(None, 2 * N_KV)
            keys_of(None, 2 * N_KV)
            with pe.Fori(0, N_KV - 1) as i:
                step(i, 2 * N_KV)
                step(i, 2 * N_KV + 1)
            step(None, STEPS - 2)
            step(None, STEPS - 1, ahead=False)
            for k in range(4):
                outputs(None, STEPS, k)
            pe.wait_ge(sem("out_added"), 4 * STEPS)
            for t in range(TILES):
                transposes(TILES + t, xn2[:, t % 2, :])

            with pe.Fori(0, PAIRS) as i:
                pe.wait_ge(sem("gateup_split"), i * 4 + 4)
                for tb in range(4):
                    toks = slice(STEP * tb, STEP * tb + STEP)
                    pe.wait_ge(sem("xnT_split"), TILES + 4 * tb + 4)
                    for t in range(2):
                        n = 2 * tb + t
                        for m, ps, ready, free in ((0, ps_s, "gate_ready", "silu_ready"),
                                                   (1, ps_p, "up_ready", "h_ready")):
                            if n >= 2:
                                pe.wait_ge(sem(free), i * 8 + (n - 1))
                            product(ps[n % 2][:], [
                                ((wf_hi[:, t, m, k * P:k * P + P], wf_lo[:, t, m, k * P:k * P + P]),
                                 (x2T_hi[:, k, toks], x2T_lo[:, k, toks])) for k in range(KC)]
                                ).then_inc(sem(ready), 1)
                pe.wait_ge(sem("down_split"), i * 2 + 2)
                for t in range(TILES):
                    pe.wait_ge(sem("h_split"), i * 8 + 2 * (t // 4) + 2)
                    if t >= 2:
                        pe.wait_ge(sem("down_added"), i * TILES + (t - 1))
                    tt = slice(t * P, t * P + P)
                    product(ps_o[t % 2][:], [
                        ((hT_hi[:, a, tt], hT_lo[:, a, tt]), (wf_hi[:, a, 2, :], wf_lo[:, a, 2, :]))
                        for a in range(2)]).then_inc(sem("down_ready"), 1)


def group(i, off):
    return i + off


def kernel(**inputs):
    import concourse.bacc as bacc
    from concourse.bass_utils import run_bass_kernel_spmd

    def by_chunk(w, rows, cols):
        return w.reshape(rows // P, P, cols).transpose(1, 0, 2).reshape(P, -1)

    a = {k: np.asarray(v) for k, v in inputs.items()}
    wq, wk, wv, wo = (a[f"L0_attn_w{k}"] for k in "qkvo")
    gd = GROUP * HD
    w_qkv = np.stack([np.concatenate([by_chunk(wv[g * HD:(g + 1) * HD].T, D, HD),
                                      by_chunk(wk[g * HD:(g + 1) * HD].T, D, HD),
                                      by_chunk(wq[g * gd:(g + 1) * gd].T, D, gd)], 1) for g in range(N_KV)])
    w_o = np.stack([by_chunk(wo.T[g * gd:(g + 1) * gd], gd, D) for g in range(N_KV)])
    codes, scales = [], []
    gq, uq, dq = (a[f"L0_ffn_{k}_q"] for k in ("gate", "up", "down"))
    ga, ua = (a[f"L0_ffn_{k}_absmax"].reshape(M_FFN, D // 64) for k in ("gate", "up"))
    da = a["L0_ffn_down_absmax"].reshape(D, M_FFN // 64)
    for t in range(MT):
        m = slice(t * P, t * P + P)
        codes.append(np.concatenate([by_chunk(gq[m].T, D, P), by_chunk(uq[m].T, D, P), dq[:, m].T], 1))
        scales.append(np.concatenate([ga[m].T.reshape(KC, 2, P).transpose(1, 0, 2).reshape(2, -1),
                                      ua[m].T.reshape(KC, 2, P).transpose(1, 0, 2).reshape(2, -1),
                                      da[:, 2 * t:2 * t + 2].T], 1))
    arrays = {"x": a["L0_attn_x"].reshape(BATCH * SEQ, D), "w_qkv": w_qkv, "w_o": w_o,
              "codes": np.stack(codes), "absmax": np.stack(scales)}
    arrays = {f"{k}_dram": np.ascontiguousarray(v) for k, v in arrays.items()}

    nc = bacc.Bacc("TRN2", target_bir_lowering=False, num_devices=1)
    args = [nc.dram_tensor(k, v.shape, mybir.dt.from_np(v.dtype), kind="ExternalInput").ap()
            for k, v in arrays.items()]
    out = nc.dram_tensor("out_dram", (BATCH * SEQ, D), F32, kind="ExternalOutput").ap()
    build(nc, *args, out)
    r = run_bass_kernel_spmd(nc, [arrays], core_ids=[0])
    return r.results[0]["out_dram"].reshape(BATCH, SEQ, D)
```

```python
from contextlib import ExitStack

import concourse.bass as bass
import concourse.mybir as mybir
import numpy as np

F32 = mybir.dt.float32
F32R = mybir.dt.float32r
I32 = mybir.dt.int32
ALU = mybir.AluOpType
ACT = mybir.ActivationFunctionType
AX = mybir.AxisListType

P = 128
BATCH, SEQ, D = 2, 1024, 512
N_KV, GROUP, HD, WINDOW = 8, 4, 128, 64
M_FFN, QBLOCK = 1792, 64
EPS = 1e-5
SCALE = float(HD) ** -0.5
MASKED = -1.0e30

KC = D // P
STEP = 512
TILES = BATCH * SEQ // P
SEQ_TILES = SEQ // P
ITS = BATCH * N_KV
STEPS = 2 * ITS
BLOCKS = STEP // QBLOCK
BANKS = BLOCKS // 2
MT = M_FFN // P
PAIRS = MT // 2
CH = 256
NF_CHUNKS = 3 * D // CH
NF_PER_STEP = NF_CHUNKS // 2
NF_ITS = MT

WARM_UP = 36

V_AT, K_AT, Q_AT = 0, KC * HD, 2 * KC * HD
QKV_COLS = Q_AT + KC * GROUP * HD
WO_COLS = GROUP * D

NF_LINES = [
    (0, 0.3038071990013123, -1.0),
    (7, 0.13015556335449219, 0.12570476531982422),
    (7, 0.09966795146465302, 0.014562472701072693),
    (7, 0.09105003625154495, 0.0),
    (8, 0.08134990185499191, 0.07958029955625534),
    (8, 0.09180293977260590, 0.06250641494989395),
    (8, 0.12190717458724976, -0.04691886901855469),
    (8, 0.27704316377639771, -0.93930214643478394),
]


def times(i, c, per, off):
    const = c * per + off
    assert const >= 0
    return const if i is None else i * (2 * per) + const


def of_pair(i, p, per, off):
    return per * p + off if i is None else i * per + (per * p + off)


def build(nc, x, w_qkv, w_o, codes, absmax, out):
    ctx = ExitStack()
    with ctx:
        w_ffn = nc.dram_tensor("w_ffn_dram", (MT, P, 3 * D), F32).ap()
        sems = {}

        def sem(name):
            if name not in sems:
                sems[name] = ctx.enter_context(nc.semaphore(name))
            return sems[name]

        def sb(stack, name, shape, dt=F32):
            return stack.enter_context(nc.sbuf_tensor(name, shape, dt))

        resid = sb(ctx, "resid", [P, TILES, D])
        ident = sb(ctx, "ident", [P, P])
        stats = sb(ctx, "stats", [P, TILES, 6])
        meanvar = sb(ctx, "meanvar", [P, TILES, 2])
        std = sb(ctx, "std", [P, TILES])
        rstd = sb(ctx, "rstd", [P, TILES])
        eps = sb(ctx, "eps", [P, 1])
        xn = sb(ctx, "xn", [P, 2, D])
        w_raw = sb(ctx, "w_raw", [P, QKV_COLS])
        wf_raw = w_raw[:].rearrange("p (t m d) -> p t m d", t=2, m=3)

        with ExitStack() as nf4:
            nf_q = sb(nf4, "nf_q", [P, 2, CH], I32)
            nf_am = sb(nf4, "nf_am", [P, 2, CH])
            nf_line = sb(nf4, "nf_line", [P, 2, 8, CH])
        wf_hi = sb(ctx, "wf_hi", [P, 2, 3, D], F32R)
        wf_lo = sb(ctx, "wf_lo", [P, 2, 3, D], F32R)

        with ExitStack() as att:
            xnT_hi = sb(att, "xnT_hi", [P, KC, SEQ], F32R)
            xnT_lo = sb(att, "xnT_lo", [P, KC, SEQ], F32R)
            qkv_hi = sb(att, "qkv_hi", [P, QKV_COLS], F32R)
            qkv_lo = sb(att, "qkv_lo", [P, QKV_COLS], F32R)
            wo_hi = sb(att, "wo_hi", [P, GROUP, D], F32R)
            wo_lo = sb(att, "wo_lo", [P, GROUP, D], F32R)
            qT = sb(att, "qT", [P, GROUP // 2, BLOCKS, 2, QBLOCK])
            kT = sb(att, "kT", [P, 2, WINDOW + STEP])
            vT = sb(att, "vT", [P, STEP])
            vtile = sb(att, "vtile", [P, 2, BLOCKS // 2, HD], F32R)
            vshift = sb(att, "vshift", [P, 2, BLOCKS, HD], F32R)
            masked_s = sb(att, "masked_s", [P, 2, 4, P])
            probs = sb(att, "probs", [P, 3, 4, P])
            pT_hi = sb(att, "pT_hi", [P, 2, 2, 2 * P], F32R)
            pT_lo = sb(att, "pT_lo", [P, 2, 2, 2 * P], F32R)
            oT_hi = sb(att, "oT_hi", [P, GROUP, STEP], F32R)
            oT_lo = sb(att, "oT_lo", [P, GROUP, STEP], F32R)
            mask = sb(att, "mask", [P, 2, P])
            rowmax = sb(att, "rowmax", [P, 2, 4])
            negmax = sb(att, "negmax", [P, 2, 4])
            rowsum = sb(att, "rowsum", [P, BANKS, 4])
            rsum = sb(att, "rsum", [P, BANKS, 4])
        with ExitStack() as ffn:
            x2T = [[sb(ffn, f"x2T{b}_{part}", [P, KC, SEQ], F32R) for part in ("hi", "lo")]
                   for b in range(BATCH)]
            hT_hi = sb(ffn, "hT_hi", [P, 2, TILES * P], F32R)
            hT_lo = sb(ffn, "hT_lo", [P, 2, TILES * P], F32R)
            silu_g = sb(ffn, "silu_g", [P, 2, STEP])
            h_full = sb(ffn, "h_full", [P, 2, STEP])

        def bank_pair(name):
            return [ctx.enter_context(nc.psum_tensor(f"{name}{k}", [P, STEP], F32)) for k in range(2)]

        ps_r, ps_s, ps_p, ps_o = (bank_pair(n) for n in ("ps_r", "ps_s", "ps_p", "ps_o"))

        def o_slot(oT, j):
            return oT[:, :, 2 * QBLOCK * j:2 * QBLOCK * (j + 1)].rearrange("p h (b q) -> p b h q", b=2)

        def o_psum(j):
            return ps_o[j % 2][:].rearrange("p (b h q) -> p b h q", b=2, h=GROUP)

        block = ctx.enter_context(nc.Block())

        @block.sync
        def _(sp):
            def load_x(t0, t1):
                sp.dma_start(resid[:, t0:t1, :],
                             x[P * t0:P * t1, :].rearrange("(t p) d -> p t d", p=P)
                             ).then_inc(sem(f"x_loaded{t0}"), 16)

            def load_qkv(i, it, g):
                sp.wait_ge(sem("wo_split"), times(i, 2 * it, 2, 0))
                sp.dma_start(w_raw[:], w_qkv[g]).then_inc(sem("raw_loaded"), 16)

            def load_wo(i, it, g):
                sp.wait_ge(sem("qkv_split"), times(i, 2 * it, 3, 6))
                sp.dma_start(w_raw[:, 0:WO_COLS], w_o[g]).then_inc(sem("raw_loaded"), 16)

            def nf_place(i, it, m):
                col = m * CH
                return (bass.ds(it if i is None else i + it, 1), slice(col, col + CH))

            def nf_load(i, it, m):
                tile, cols = nf_place(i, it, m)
                if i is not None or it or m >= 2:
                    sp.wait_ge(sem("nf_lines_done"), times(i, 2 * it, NF_PER_STEP, m - 1))
                    sp.wait_ge(sem("nf_dequantised"), times(i, 2 * it, NF_PER_STEP, m - 1))
                loaded = sem(f"nf_loaded{m % 2}")
                sp.dma_start(nf_q[:, m % 2, :], codes[tile, :, cols].rearrange("o p c -> (o p) c")
                             ).then_inc(loaded, 16)
                for half in range(2):
                    sp.dma_start(nf_am[64 * half:64 * half + 64, m % 2, :],
                                 absmax[tile, half, cols].broadcast_to([64, CH])).then_inc(loaded, 16)

            def nf_store(i, it, m):
                tile, cols = nf_place(i, it, m)
                sp.wait_ge(sem("nf_dequantised"), times(i, 2 * it, NF_PER_STEP, m + 1))
                sp.dma_start(w_ffn[tile, :, cols].rearrange("o p c -> (o p) c"),
                             nf_line[:, m % 2, 0, :]).then_inc(sem(f"nf_stored{m % 2}"), 16)

            def iteration(i, it, g, next_g, nf):
                if nf:
                    nf_load(i, it, 0)
                    if i is not None or it:
                        nf_store(i, it - 1, NF_CHUNKS - 1)
                load_wo(i, it, g)
                for m in range(1, NF_CHUNKS) if nf else ():
                    nf_load(i, it, m)
                    if m == NF_CHUNKS - 1 and next_g is not None:
                        load_qkv(i, it + 1, next_g)
                    nf_store(i, it, m - 1)
                if not nf and next_g is not None:
                    load_qkv(i, it + 1, next_g)

            for t in range(4):
                load_x(t, t + 1)
            sp.dma_start(w_raw[:, 0:Q_AT], w_qkv[0, :, 0:Q_AT]).then_inc(sem("first_vk_loaded"), 16)
            load_x(4, 8)
            sp.dma_start(w_raw[:, Q_AT:], w_qkv[0, :, Q_AT:]).then_inc(sem("raw_loaded"), 16)
            load_x(8, 16)
            iteration(None, 0, 0, 1, True)
            with sp.Fori(0, N_KV - 2) as i:
                iteration(i, 1, group(i, 1), group(i, 2), True)
            iteration(None, N_KV - 1, N_KV - 1, 0, True)
            with sp.Fori(0, NF_ITS - N_KV) as i:
                iteration(i, N_KV, group(i, 0), group(i, 1), True)
            nf_store(None, NF_ITS - 1, NF_CHUNKS - 1)
            iteration(None, NF_ITS, NF_ITS - N_KV, NF_ITS - N_KV + 1, False)
            iteration(None, NF_ITS + 1, N_KV - 1, None, False)

            for k in range(2):
                sp.wait_ge(sem(f"nf_stored{k}"), 16 * MT * NF_CHUNKS // 2)
            sp.wait_ge(sem("wo_split"), 4 * ITS)
            for i in range(PAIRS):
                if i:
                    sp.wait_ge(sem("gateup_split"), i * 4)
                    sp.wait_ge(sem("down_split"), i * 2)
                sp.dma_start(wf_raw, w_ffn[2 * i:2 * i + 2].rearrange(
                    "t p (m d) -> p t m d", m=3)).then_inc(sem("wf_loaded"), 16)
            for t in range(TILES):
                sp.wait_ge(sem("down_added"), TILES * (PAIRS - 1) + t + 1)
                sp.dma_start(out[t * P:(t + 1) * P, :], resid[:, t, :]).then_inc(sem("stored"), 16)
            sp.wait_ge(sem("stored"), 16 * TILES)

        @block.gpsimd
        def _(pool):
            pool.memset(ident[:], 0.0).then_inc(sem("ident_zero"), 1)
            pool.wait_ge(sem("ident_zero"), 1)
            pool.affine_select(out=ident[:], in_=ident[:], compare_op=ALU.not_equal, fill=1.0, base=0,
                               pattern=[[-1, P]], channel_multiplier=1).then_inc(sem("ident_ready"), 1)
            pool.memset(mask[:], 0.0).then_inc(sem("mask_zero"), 1)
            pool.memset(kT[:, 0, 0:WINDOW], 0.0)
            pool.memset(vshift[:, :, 0, :].bitcast(F32), 0.0).then_inc(sem("pad_zero"), 1)
            pool.wait_ge(sem("mask_zero"), 1)
            pool.wait_ge(sem("pad_zero"), 1)
            for h in range(2):
                m = mask[64 * h:64 * h + 64, :, :]
                pool.affine_select(out=m, in_=m, compare_op=ALU.is_ge, fill=MASKED, base=-1,
                                   pattern=[[0, 2], [1, P]], channel_multiplier=-1
                                   ).then_inc(sem("mask_low"), 1)
                pool.wait_ge(sem("mask_low"), h + 1)
            for h in range(2):
                m = mask[64 * h:64 * h + 64, :, :]
                pool.affine_select(out=m, in_=m, compare_op=ALU.is_ge, fill=MASKED, base=WINDOW,
                                   pattern=[[0, 2], [-1, P]], channel_multiplier=1
                                   ).then_inc(sem("mask_high"), 1)
                pool.wait_ge(sem("mask_high"), h + 1)
            pool.memset(mask[:, 0, 0:WINDOW], MASKED).then_inc(sem("mask_ready"), 1)

            def waits_end():
                pool.sem_inc(sem("pool_waits"), 1)

            def split_qkv(i, it, at, to):
                last = QKV_COLS // 512
                if i is None and it == 0:
                    pool.wait_ge(sem("raw_loaded" if at else "first_vk_loaded"), 16)
                elif at == 0:
                    pool.wait_ge(sem("raw_loaded"), times(i, 2 * it, 16, 16))
                    if i is not None or it > 0:
                        pool.wait_ge(sem("proj_ready"), times(i, 2 * it, 6, 0))
                for k in range(at, to):
                    cols = slice(512 * k, 512 * k + 512)
                    if k == at:
                        waits_end()
                    pool.tensor_scalar(qkv_hi[:, cols], w_raw[:, cols], 1.0, 0.0, ALU.mult, ALU.add
                                       ).then_inc(sem("qkv_rounded"), 1)
                    pool.wait_ge(sem("qkv_rounded"), times(i, 2 * it, last // 2, k + 1))
                    pool.tensor_tensor(qkv_lo[:, cols], w_raw[:, cols], qkv_hi[:, cols].bitcast(F32),
                                       ALU.subtract).then_inc(sem("qkv_split"), 1)

            def split_wo(i, it):
                pool.wait_ge(sem("raw_loaded"), times(i, 2 * it, 16, 32))
                if i is not None or it > 0:
                    pool.wait_ge(sem("out_ready"), times(i, 2 * it, 4, 0))
                waits_end()
                for k in range(GROUP):
                    raw = w_raw[:, D * k:D * k + D]
                    pool.tensor_scalar(wo_hi[:, k, :], raw, 1.0, 0.0, ALU.mult, ALU.add
                                       ).then_inc(sem("wo_rounded"), 1)
                    pool.wait_ge(sem("wo_rounded"), times(i, 2 * it, GROUP // 2, k + 1))
                    pool.tensor_tensor(wo_lo[:, k, :], raw, wo_hi[:, k, :].bitcast(F32),
                                       ALU.subtract).then_inc(sem("wo_split"), 1)

            def nf_lines(i, it, m):
                q = nf_q[:, m % 2, :]
                pool.wait_ge(sem(f"nf_loaded{m % 2}"), times(i, 2 * it, 72, 48 * (m // 2 + 1)))
                if i is not None or it or m >= 2:
                    pool.wait_ge(sem(f"nf_stored{m % 2}"), times(i, 2 * it, 24, 16 * (m // 2)))
                waits_end()
                L = [nf_line[:, m % 2, j, :] for j in range(8)]
                pool.tensor_scalar(L[3], q, 1.0, -7.0, ALU.mult, ALU.add).then_inc(sem("nf_shifted"), 1)
                pool.tensor_scalar(L[7], q, 1.0, -8.0, ALU.mult, ALU.add).then_inc(sem("nf_shifted"), 1)
                pool.wait_ge(sem("nf_shifted"), times(i, 2 * it, NF_CHUNKS, 2 * (m + 1)))
                waits_end()
                for j in (0, 1, 2, 4, 5, 6):
                    shift, slope, intercept = NF_LINES[j]
                    last = pool.tensor_scalar(L[j], {0: q, 7: L[3], 8: L[7]}[shift], slope, intercept,
                                              ALU.mult, ALU.add)
                last.then_inc(sem("nf_six_lines"), 1)
                pool.wait_ge(sem("nf_six_lines"), times(i, 2 * it, NF_PER_STEP, m + 1))
                waits_end()
                for j in (3, 7):
                    _, slope, intercept = NF_LINES[j]
                    last = pool.tensor_scalar(L[j], L[j], slope, intercept, ALU.mult, ALU.add)
                last.then_inc(sem("nf_lines_done"), 1)

            def normalise(i, c, j):
                pool.wait_ge(sem("rsum_ready"), times(i, c, 4, j + 1))
                p = probs[:, j % 3]
                pool.tensor_tensor(p, p, rsum[:, j, :, None].broadcast_to([P, 4, P]),
                                   ALU.mult).then_inc(sem("normalised"), 1)

            def iteration(i, it, nf, next_nf, last=False):
                c = 2 * it
                for m in range(1, NF_PER_STEP) if nf else ():
                    nf_lines(i, it, m)
                for j in range(BANKS):
                    normalise(i, c, j)
                if nf:
                    nf_lines(i, it, NF_PER_STEP)
                split_wo(i, it)
                for m in range(NF_PER_STEP + 1, NF_CHUNKS) if nf else ():
                    nf_lines(i, it, m)
                if not last:
                    split_qkv(i, it + 1, 0, 2)
                for j in range(BANKS):
                    normalise(i, c + 1, j)
                    if not last and j:
                        split_qkv(i, it + 1, (2, 4, 5)[j - 1], (4, 5, 6)[j - 1])
                if next_nf:
                    nf_lines(i, it + 1, 0)

            split_qkv(None, 0, 0, 2)
            split_qkv(None, 0, 2, QKV_COLS // 512)
            nf_lines(None, 0, 0)
            iteration(None, 0, True, True)
            with pool.Fori(0, NF_ITS - 2) as i:
                iteration(i, 1, True, True)
            iteration(None, NF_ITS - 1, True, False)
            iteration(None, NF_ITS, False, False)
            iteration(None, NF_ITS + 1, False, False, last=True)

            def split_wf(i, off, kinds, name):
                n = 2 * len(kinds)
                waits_end()
                for a, (t, m) in enumerate((t, m) for t in range(2) for m in kinds):
                    raw = wf_raw[:, t, m, :]
                    pool.tensor_scalar(wf_hi[:, t, m, :], raw, 1.0, 0.0, ALU.mult, ALU.add
                                       ).then_inc(sem(name + "_rounded"), 1)
                    pool.wait_ge(sem(name + "_rounded"), (off * n + a + 1) if i is None else i * n + (off * n + a + 1))
                    pool.tensor_tensor(wf_lo[:, t, m, :], raw, wf_hi[:, t, m, :].bitcast(F32),
                                       ALU.subtract).then_inc(sem(name + "_split"), 1)

            def wf_down(i, off):
                split_wf(i, off, (2,), "down")

            def round_h(i, off):
                for n in range(8):
                    tb, t = n // 2, n % 2
                    pool.wait_ge(sem("h_ready"), (8 * off + n + 1) if i is None else i * 8 + (8 * off + n + 1))
                    waits_end()
                    pool.tensor_scalar(hT_hi[:, t, STEP * tb:STEP * tb + STEP], h_full[:, t, :],
                                       1.0, None, ALU.mult).then_inc(sem("h_rounded"), 1)

            pool.wait_ge(sem("wf_loaded"), 16)
            split_wf(None, 0, (0, 1), "gateup")
            wf_down(None, 0)
            with pool.Fori(0, PAIRS - 1) as i:
                round_h(i, 0)
                pool.wait_ge(sem("wf_loaded"), i * 16 + 32)
                pool.wait_ge(sem("up_ready"), i * 8 + 8)
                split_wf(i, 1, (0, 1), "gateup")
                pool.wait_ge(sem("down_ready"), i * TILES + TILES)
                wf_down(i, 1)
            round_h(None, PAIRS - 1)

        @block.scalar
        def _(act):
            def copy(out_, in_):
                return act.activation(out_, in_, ACT.Copy)

            def stds(t0, t1, n):
                act.wait_ge(sem("var_ready"), n)
                act.wait_ge(sem("eps_ready"), 1)
                act.activation(std[:, t0:t1], meanvar[:, t0:t1, 1], ACT.Sqrt, bias=eps[:, 0:1]
                               ).then_inc(sem("std_ready"), 1)

            def norm_hi(n, hi, ps, at):
                act.wait_ge(sem("xnT_ready"), n + 1)
                copy(hi[:, :, at * P:at * P + P],
                     ps[n % 2][:].rearrange("p (k t) -> p k t", k=KC)).then_inc(sem("xnT_rounded"), 1)

            def norm1_hi(t):
                norm_hi(t, xnT_hi, ps_s, t % SEQ_TILES)

            def norm2_hi(t):
                norm_hi(TILES + t, x2T[t // SEQ_TILES][0], ps_s if t < 4 else ps_r, t % SEQ_TILES)

            def step(i, c, first=False, extra={}):
                u = c % 2

                def point(name):
                    for f, t in extra.get(name, ()):
                        f(t)

                act.wait_ge(sem("proj_ready"), times(i, c, 6, 1))
                if not first:
                    act.wait_ge(sem("vtile_ready"), times(i, c, 1, 0))
                else:
                    act.wait_ge(sem("pad_zero"), 1)
                copy(vT[:], ps_r[0][:]).then_inc(sem("v_copied"), 1)
                act.wait_ge(sem("proj_ready"), times(i, c, 6, 2))
                if not first:
                    act.wait_ge(sem("score_ready"), times(i, c, 4, 0))
                ps = ps_r[1]
                if u == 0:
                    copy(kT[:, 1, 0:WINDOW], ps[:, STEP - WINDOW:STEP])
                copy(kT[:, u, WINDOW:], ps[:]).then_inc(sem("qk_copied"), 1)
                point("keys")
                for h in range(GROUP):
                    act.wait_ge(sem("proj_ready"), times(i, c, 6, 3 + h))
                    copy(qT[:, h // 2, :, h % 2, :], ps_r[h % 2][:].rearrange(
                        "p (b q) -> p b q", b=BLOCKS)).then_inc(sem("qk_copied"), 1)
                    if h == 0:
                        act.wait_ge(sem("vtile_ready"), times(i, c, 1, 1))
                        if not first:
                            act.wait_ge(sem("pv_ready"), times(i, c, 4, 0))
                        copy(vtile[:, 0], ps_p[0][:].rearrange("p (w d) -> p w d", w=4)
                             ).then_inc(sem("vtile_rounded"), 1)
                        point("query0")
                    if h == 1:
                        act.wait_ge(sem("vtile_split"), times(i, c, 1, 1))
                        n = 4 - u
                        act.dma_start(vshift[0:64, :, 4 * u + 1:4 * u + 1 + n, :].bitcast(F32),
                                      vtile[64:128, :, 0:n, :].bitcast(F32)
                                      ).then_inc(sem("v_shifted"), 16)
                        act.dma_start(vshift[64:128, :, 4 * u:4 * u + 4, :].bitcast(F32),
                                      vtile[0:64].bitcast(F32)).then_inc(sem("v_shifted"), 16)

                def exps(j):
                    act.wait_ge(sem("negmax_ready"), times(i, c, 4, j + 1))
                    if j == 3 or not first:
                        act.wait_ge(sem("pT_ready"), times(i, c, 4, j // 3))
                    for t in range(4):
                        last = act.activation(probs[:, j % 3, t, :], masked_s[:, j % 2, t, :], ACT.Exp,
                                              bias=negmax[:, j % 2, t:t + 1], scale=SCALE,
                                              accum_out=rowsum[:, j, t:t + 1])
                    last.then_inc(sem("exp_done"), 1)

                def pT(j):
                    act.wait_ge(sem("pT_ready"), times(i, c, 4, j + 1))
                    if not first or j >= 2:
                        act.wait_ge(sem("pv_ready"), times(i, c, 4, j - 1))
                    copy(pT_hi[:, j % 2], ps_p[j % 2][:].rearrange("p (b q) -> p b q", b=2)
                         ).then_inc(sem("pT_rounded"), 1)

                def oT(j):
                    act.wait_ge(sem("pv_ready"), times(i, c, 4, j + 1))
                    if not first:
                        act.wait_ge(sem("out_ready"), times(i, c - 1, 4, j + 1))
                    copy(o_slot(oT_hi, j), o_psum(j)).then_inc(sem("oT_rounded"), 1)

                exps(0)
                exps(1)
                exps(2)
                pT(0)
                pT(1)
                exps(3)
                oT(0)
                pT(2)
                oT(1)
                point("values1")
                pT(3)
                oT(2)
                point("values2")
                oT(3)
                point("values3")

            def second_half(t):
                return {"keys": [(norm1_hi, t + 4), (norm1_hi, t + 5)],
                        "query0": [(norm1_hi, t + 6), (norm1_hi, t + 7)]}

            stds(0, 4, 4)
            for t in range(4):
                norm1_hi(t)
            stds(4, SEQ_TILES, SEQ_TILES)
            step(None, 0, True, extra=second_half(0))
            step(None, 1)
            with act.Fori(0, N_KV - 2) as i:
                step(i, 2)
                step(i, 3)
            step(None, 2 * N_KV - 2)
            stds(SEQ_TILES, TILES, TILES)
            t = SEQ_TILES
            step(None, 2 * N_KV - 1, extra={
                "values1": [(norm1_hi, t)],
                "values2": [(norm1_hi, t + 1), (norm1_hi, t + 2), (norm1_hi, t + 3)]})
            step(None, 2 * N_KV, extra=second_half(t))
            step(None, 2 * N_KV + 1)
            with act.Fori(0, NF_ITS - N_KV - 1) as i:
                step(i, 2 * N_KV + 2)
                step(i, 2 * N_KV + 3)
            step(None, 2 * NF_ITS)
            step(None, 2 * NF_ITS + 1)
            stds(0, SEQ_TILES, TILES + SEQ_TILES)
            step(None, STEPS - 2)
            step(None, STEPS - 1, extra={"values2": [(norm2_hi, 0)], "values3": [(norm2_hi, 1)]})
            stds(SEQ_TILES, SEQ_TILES + 4, TILES + SEQ_TILES + 4)
            norm2_hi(2)
            norm2_hi(3)

            def silu(i, p, n):
                act.wait_ge(sem("gate_ready"), of_pair(i, p, 8, n + 1))
                if n >= 2:
                    act.wait_ge(sem("h_ready"), of_pair(i, p, 8, n - 1))
                act.activation(silu_g[:, n % 2, :], ps_s[n % 2][:], ACT.Silu
                               ).then_inc(sem("silu_ready"), 1)

            for tb in range(4):
                t = 4 * tb + 4
                silu(None, 0, 2 * tb)
                if tb == 1:
                    stds(12, 16, 2 * TILES)
                if tb < 3:
                    norm2_hi(t)
                    norm2_hi(t + 1)
                silu(None, 0, 2 * tb + 1)
                if tb < 3:
                    norm2_hi(t + 2)
                    norm2_hi(t + 3)
            with act.Fori(0, PAIRS - 1) as i:
                for n in range(8):
                    silu(i, 1, n)

        @block.vector
        def _(dve):
            def variances(t, n):
                dve.bn_stats(stats[:, t, :], resid[:, t, :]).then_inc(sem("stats_ready"), 1)
                dve.wait_ge(sem("stats_ready"), n + 1)
                dve.bn_aggr(meanvar[:, t, :], stats[:, t, :]).then_inc(sem("var_ready"), 1)

            def rstds(t0, t1, n):
                dve.wait_ge(sem("std_ready"), n)
                dve.reciprocal(rstd[:, t0:t1], std[:, t0:t1]).then_inc(sem("rstd_ready"), 1)

            def normalise(t, n, r):
                dve.wait_ge(sem("rstd_ready"), r)
                if n >= 2:
                    dve.wait_ge(sem("xnT_ready"), n - 1)
                dve.tensor_scalar(xn[:, n % 2, :], resid[:, t, :], meanvar[:, t, 0:1], rstd[:, t:t + 1],
                                  ALU.subtract, ALU.mult).then_inc(sem("xn_ready"), 1)

            def norm_lo(n, lo, hi, ps, at):
                dve.wait_ge(sem("xnT_rounded"), n + 1)
                cols = slice(at * P, at * P + P)
                dve.tensor_tensor(lo[:, :, cols], ps[n % 2][:].rearrange("p (k t) -> p k t", k=KC),
                                  hi[:, :, cols].bitcast(F32), ALU.subtract
                                  ).then_inc(sem("xnT_split"), 1)

            def normalise1(t):
                normalise(t, t, min(t // 4, 2) + 1)

            def norm1_lo(t):
                norm_lo(t, xnT_lo, xnT_hi, ps_s, t % SEQ_TILES)

            def normalise2(t):
                normalise(t, TILES + t, 3 + max(t // 4, 1))

            def norm2_lo(t):
                hi, lo = x2T[t // SEQ_TILES]
                norm_lo(TILES + t, lo, hi, ps_s if t < 4 else ps_r, t % SEQ_TILES)

            def rest(lo, ps, hi):
                return dve.tensor_tensor(lo, ps, hi.bitcast(F32), ALU.subtract)

            def nf_least(i, it, m):
                L = [nf_line[:, m % 2, j, :] for j in range(8)]
                dve.wait_ge(sem("nf_lines_done"), times(i, 2 * it, NF_PER_STEP, m + 1))
                dve.scalar_tensor_tensor(L[0], L[0], 0.0, L[1], ALU.min, ALU.min)
                dve.tensor_tensor(L[2], L[2], L[3], ALU.min)
                dve.scalar_tensor_tensor(L[4], L[4], 0.0, L[5], ALU.max, ALU.max)
                dve.tensor_tensor(L[6], L[6], L[7], ALU.max).then_inc(sem("nf_quarters"), 1)

            def nf_combine(i, it, m):
                L = [nf_line[:, m % 2, j, :] for j in range(8)]
                dve.wait_ge(sem("nf_quarters"), times(i, 2 * it, NF_PER_STEP, m + 1))
                dve.tensor_tensor(L[1], L[0], L[2], ALU.min)
                dve.tensor_tensor(L[5], L[4], L[6], ALU.max).then_inc(sem("nf_halves"), 1)
                dve.wait_ge(sem("nf_halves"), times(i, 2 * it, NF_PER_STEP, m + 1))
                dve.tensor_tensor(L[3], L[1], L[5], ALU.add).then_inc(sem("nf_coded"), 1)
                dve.wait_ge(sem("nf_coded"), times(i, 2 * it, NF_PER_STEP, m + 1))
                dve.tensor_tensor(L[0], L[3], nf_am[:, m % 2, :], ALU.mult
                                  ).then_inc(sem("nf_dequantised"), 1)

            def step(i, c, nf, first=False, ahead=True, extra={}):
                u = c % 2

                def point(name):
                    for f, t in extra.get(name, ()):
                        f(t)

                def values_lo():
                    dve.wait_ge(sem("vtile_rounded"), times(i, c, 1, 1))
                    rest(vtile[:, 1], ps_p[0][:].rearrange("p (w d) -> p w d", w=4),
                         vtile[:, 0]).then_inc(sem("vtile_split"), 1)

                def softmax(j):
                    dve.wait_ge(sem("score_ready"), times(i, c, 4, j + 1))
                    if not first or j >= 2:
                        dve.wait_ge(sem("exp_done"), times(i, c, 4, j - 1))
                    m = mask[:, 0:2] if u == 0 and j == 0 else mask[:, 1:2].broadcast_to([P, 2, P])
                    s = masked_s[:, j % 2]
                    dve.tensor_tensor(s.rearrange("p (b g) k -> p b g k", b=2),
                                      ps_s[j % 2][:].rearrange("p (b g k) -> p b g k", b=2, g=2),
                                      m[:, :, None, :].broadcast_to([P, 2, 2, P]),
                                      ALU.add).then_inc(sem("masked"), 1)
                    dve.wait_ge(sem("masked"), times(i, c, 4, j + 1))
                    dve.tensor_reduce(rowmax[:, j % 2, :], s, AX.X, ALU.max).then_inc(sem("max_ready"), 1)
                    dve.wait_ge(sem("max_ready"), times(i, c, 4, j + 1))
                    dve.tensor_scalar(negmax[:, j % 2, :], rowmax[:, j % 2, :], -SCALE, None, ALU.mult
                                      ).then_inc(sem("negmax_ready"), 1)

                def recip(j):
                    dve.wait_ge(sem("exp_done"), times(i, c, 4, j + 1))
                    if not first:
                        dve.wait_ge(sem("normalised"), times(i, c, 4, 0))
                    dve.reciprocal(rsum[:, j, :], rowsum[:, j, :]).then_inc(sem("rsum_ready"), 1)

                def pT(j):
                    dve.wait_ge(sem("pT_rounded"), times(i, c, 4, j + 1))
                    rest(pT_lo[:, j % 2], ps_p[j % 2][:].rearrange("p (b q) -> p b q", b=2), pT_hi[:, j % 2]
                         ).then_inc(sem("pT_split"), 1)

                def oT(j):
                    dve.wait_ge(sem("oT_rounded"), times(i, c, 4, j + 1))
                    rest(o_slot(oT_lo, j), o_psum(j), o_slot(oT_hi, j)).then_inc(sem("oT_split"), 1)

                def add_out(k):
                    if not first:
                        residual(i, c, k)

                def nf_parts(parts):
                    for k in parts if nf else ():
                        (nf_combine if k % 2 else nf_least)(i, c // 2, u * NF_PER_STEP + k // 2)

                nf_start, nf_windows, nf_probs, nf_end = (
                    ((), (0, 1), (2, 3), (4, 5)), ((0, 1), (2, 3), (4, 5), ()), ((0, 1), (2, 3, 4), (5,), ())
                )[2 if i is not None else min(c % (2 * N_KV), 2)]
                point("start")
                nf_parts(nf_start)
                values_lo()
                point("windows")
                nf_parts(nf_windows)
                softmax(0)
                softmax(1)
                add_out(0)
                recip(0)
                softmax(2)
                recip(1)
                softmax(3)
                recip(2)
                add_out(1)
                pT(0)
                pT(1)
                nf_parts(nf_probs)
                add_out(2)
                recip(3)
                oT(0)
                pT(2)
                oT(1)
                if ahead:
                    add_out(3)
                point("values1")
                pT(3)
                oT(2)
                point("values2")
                if not ahead:
                    add_out(3)
                oT(3)
                nf_parts(nf_end)
                point("values3")

            def residual(i, c, k):
                dve.wait_ge(sem("out_ready"), times(i, c - 1, 4, k + 1))
                u = (c - 1) % 2
                seq = 0 if c - 1 < STEPS // 2 else SEQ_TILES
                r = resid[:, seq + 4 * u + k, :]
                dve.tensor_tensor(r, ps_r[k % 2][:], r, ALU.add).then_inc(sem("out_added"), 1)

            def variances_of(t0, t1, before):
                return [(lambda t: variances(t, before + t), t) for t in range(t0, t1)]

            def second_half(t):
                return {"start": [(norm1_lo, t + 4), (norm1_lo, t + 5), (normalise1, t + 6),
                                  (normalise1, t + 7), (norm1_lo, t + 6), (norm1_lo, t + 7)]}

            dve.memset(eps[:], EPS).then_inc(sem("eps_ready"), 1)
            for t in range(4):
                dve.wait_ge(sem(f"x_loaded{t}"), 16)
                variances(t, t)
            rstds(0, 4, 1)
            for t in range(4):
                normalise1(t)
                if t:
                    norm1_lo(t - 1)
            norm1_lo(3)
            dve.wait_ge(sem("x_loaded4"), 16)
            for t in range(4, SEQ_TILES):
                variances(t, t)
            rstds(4, SEQ_TILES, 2)
            normalise1(4)
            normalise1(5)
            dve.wait_ge(sem("x_loaded8"), 16)
            step(None, 0, True, True, extra={**second_half(0), "values3": variances_of(8, 12, 0)})
            step(None, 1, True)
            with dve.Fori(0, N_KV - 2) as i:
                step(i, 2, True)
                step(i, 3, True)
            step(None, 2 * N_KV - 2, True,
                 extra={"start": variances_of(12, 14, 0), "windows": variances_of(14, 16, 0)})
            rstds(SEQ_TILES, TILES, 3)
            t = SEQ_TILES
            step(None, 2 * N_KV - 1, True, ahead=False, extra={
                "start": [(normalise1, t), (normalise1, t + 1)],
                "values1": [(norm1_lo, t), (normalise1, t + 2)],
                "values2": [(norm1_lo, t + 1), (normalise1, t + 3), (norm1_lo, t + 2), (norm1_lo, t + 3)],
                "values3": [(normalise1, t + 4), (normalise1, t + 5)]})
            step(None, 2 * N_KV, True, extra=second_half(t))
            step(None, 2 * N_KV + 1, True)
            with dve.Fori(0, NF_ITS - N_KV - 1) as i:
                step(i, 2 * N_KV + 2, True)
                step(i, 2 * N_KV + 3, True)
            dve.wait_ge(sem("out_added"), 4 * STEPS // 2)
            step(None, 2 * NF_ITS, False, extra={"start": variances_of(0, 4, TILES)})
            step(None, 2 * NF_ITS + 1, False, extra={"start": variances_of(4, 8, TILES)})
            step(None, STEPS - 2, False)
            rstds(0, SEQ_TILES, 4)
            step(None, STEPS - 1, False, ahead=False, extra={
                "start": [(normalise2, 0), (normalise2, 1)],
                "values2": [(norm2_lo, 0), (normalise2, 2)],
                "values3": [(norm2_lo, 1), (normalise2, 3)]})

            def second_variances(t0, count):
                dve.wait_ge(sem("out_added"), count)
                for t in range(t0, t0 + 4):
                    variances(t, TILES + t)

            second_variances(SEQ_TILES, 4 * (STEPS - 1))
            residual(None, STEPS, 0)
            residual(None, STEPS, 1)
            norm2_lo(2)
            norm2_lo(3)
            normalise2(4)
            normalise2(5)
            residual(None, STEPS, 2)
            residual(None, STEPS, 3)
            rstds(SEQ_TILES, SEQ_TILES + 4, 5)
            second_variances(SEQ_TILES + 4, 4 * STEPS)

            def inner(i, p, n):
                dve.wait_ge(sem("up_ready"), of_pair(i, p, 8, n + 1))
                dve.wait_ge(sem("silu_ready"), of_pair(i, p, 8, n + 1))
                if n >= 2:
                    dve.wait_ge(sem("h_split"), of_pair(i, p, 8, n - 1))
                dve.tensor_tensor(h_full[:, n % 2, :], ps_p[n % 2][:], silu_g[:, n % 2, :], ALU.mult
                                  ).then_inc(sem("h_ready"), 1)

            def inner_lo(i, p, n):
                cols = slice(STEP * (n // 2), STEP * (n // 2) + STEP)
                dve.wait_ge(sem("h_rounded"), of_pair(i, p, 8, n + 1))
                dve.tensor_tensor(hT_lo[:, n % 2, cols], h_full[:, n % 2, :],
                                  hT_hi[:, n % 2, cols].bitcast(F32), ALU.subtract
                                  ).then_inc(sem("h_split"), 1)

            def down(i, p, t0, t1):
                for t in range(t0, t1):
                    dve.wait_ge(sem("down_ready"), of_pair(i, p, TILES, t + 1))
                    r = resid[:, t, :]
                    dve.tensor_tensor(r, ps_o[t % 2][:], r, ALU.add).then_inc(sem("down_added"), 1)

            for tb in range(4):
                t = 4 * tb + 4
                if tb < 3:
                    norm2_lo(t)
                    normalise2(t + 2)
                inner(None, 0, 2 * tb)
                if tb < 3:
                    norm2_lo(t + 1)
                    normalise2(t + 3)
                inner_lo(None, 0, 2 * tb)
                if tb < 3:
                    norm2_lo(t + 2)
                    norm2_lo(t + 3)
                if tb == 1:
                    rstds(12, 16, 6)
                if tb < 2:
                    normalise2(t + 4)
                    normalise2(t + 5)
                inner(None, 0, 2 * tb + 1)
                if tb == 3:
                    down(None, 0, 0, 1)
                inner_lo(None, 0, 2 * tb + 1)
            down(None, 0, 1, TILES)
            with dve.Fori(0, PAIRS - 1) as i:
                for n in range(8):
                    inner(i, 1, n)
                    if n:
                        inner_lo(i, 1, n - 1)
                down(i, 1, 0, 1)
                inner_lo(i, 1, 7)
                down(i, 1, 1, TILES)

        @block.tensor
        def _(pe):
            def product(ps, parts):
                n = 3 * len(parts)
                a = 0
                for (s_hi, s_lo), (m_hi, m_lo) in parts:
                    for s, m in ((s_hi, m_hi), (s_hi, m_lo), (s_lo, m_hi)):
                        last = pe.matmul(ps, s, m, start=(a == 0), stop=(a == n - 1))
                        a += 1
                return last

            def transposes(n, ps):
                pe.wait_ge(sem("xn_ready"), n + 1)
                if n >= 2:
                    pe.wait_ge(sem("xnT_split"), n - 1)
                for k in range(KC):
                    last = pe.transpose(ps[n % 2][:, k * P:k * P + P], xn[:, n % 2, k * P:k * P + P], ident[:])
                last.then_inc(sem("xnT_ready"), 1)

            def tile1(t):
                if t in (SEQ_TILES, SEQ_TILES + 1):
                    pe.wait_ge(sem("masked"), 4 * STEPS // 2 - 1 + t % 2)
                transposes(t, ps_s)

            def tile2(t):
                if t < 2:
                    pe.wait_ge(sem("masked"), 4 * STEPS - 1 + t)
                transposes(TILES + t, ps_s if t < 4 else ps_r)

            def project(i, c, at, width, cols, bank):
                toks = slice(STEP * (c % 2), STEP * (c % 2) + STEP)

                def part(w, k):
                    a = at + k * width + cols
                    return w[:, a:a + HD]
                product(ps_r[bank][:], [
                    ((part(qkv_hi, k), part(qkv_lo, k)), (xnT_hi[:, k, toks], xnT_lo[:, k, toks]))
                    for k in range(KC)]).then_inc(sem("proj_ready"), 1)

            def values_of(i, c):
                if c % 2 == 0:
                    pe.wait_ge(sem("qkv_split"), times(i, c, 3, 1))
                if i is not None or c >= 2:
                    pe.wait_ge(sem("out_added"), times(i, c - 2, 4, 3))
                project(i, c, V_AT, HD, 0, 0)

            def keys_of(i, c):
                if i is not None or c >= 2:
                    pe.wait_ge(sem("out_added"), times(i, c - 2, 4, 4))
                if c % 2 == 0:
                    pe.wait_ge(sem("qkv_split"), times(i, c, 3, 2))
                project(i, c, K_AT, HD, 0, 1)

            def step(i, c, first=False, ahead=True, extra={}):
                u = c % 2

                def point(name):
                    for f, t in extra.get(name, ()):
                        f(t)

                def value_tiles():
                    if not first:
                        pe.wait_ge(sem("pT_split"), times(i, c, 4, -1))
                    for a in range(4):
                        last = pe.transpose(ps_p[0][:, a * HD:a * HD + HD], vT[:, a * P:a * P + P], ident[:])
                    last.then_inc(sem("vtile_ready"), 1)

                point("keys")
                for h in range(GROUP):
                    if h == 0:
                        pe.wait_ge(sem("v_copied"), times(i, c, 1, 1))
                        if u == 0:
                            pe.wait_ge(sem("qkv_split"), times(i, c, 3, 6))
                    else:
                        pe.wait_ge(sem("qk_copied"), times(i, c, 5, h))
                    project(i, c, Q_AT, GROUP * HD, h * HD, h % 2)
                    if h == 0:
                        value_tiles()
                        point("query0")

                def scores(j, g):
                    if g == 0 and (not first or j >= 2):
                        pe.wait_ge(sem("masked"), times(i, c, 4, j - 1))
                    if g == 0 and j < 2 and i is None and c % (2 * N_KV) == 0:
                        pe.wait_ge(sem("xnT_split"), SEQ_TILES * (c // (2 * N_KV) + 1))
                    for b in range(2):
                        keys = slice(QBLOCK * (2 * j + b), QBLOCK * (2 * j + b) + 2 * WINDOW)
                        at = (2 * b + g) * P
                        last = pe.matmul(ps_s[j % 2][:, at:at + P],
                                         qT[:, g, 2 * j + b].rearrange("p h q -> p (h q)"),
                                         kT[:, u, keys], start=True, stop=True)
                    if g == 1:
                        last.then_inc(sem("score_ready"), 1)

                def probs_T(j):
                    pe.wait_ge(sem("normalised"), times(i, c, 4, j + 1))
                    if j >= 2:
                        pe.wait_ge(sem("pT_split"), times(i, c, 4, j - 1))
                    elif j == 0:
                        pe.wait_ge(sem("vtile_split"), times(i, c, 1, 1))
                    elif not first:
                        pe.wait_ge(sem("pT_split"), times(i, c, 4, 0))
                    for t in range(4):
                        last = pe.transpose(ps_p[j % 2][:, t * P:t * P + P], probs[:, j % 3, t, :], ident[:])
                    last.then_inc(sem("pT_ready"), 1)

                def values(j):
                    pe.wait_ge(sem("pT_split"), times(i, c, 4, j + 1))
                    pe.wait_ge(sem("v_shifted"), times(i, c, 32, 32))
                    if not first or j >= 2:
                        pe.wait_ge(sem("oT_split"), times(i, c, 4, j - 1))
                    for b in range(2):
                        last = product(ps_o[j % 2][:, b * 2 * P:(b + 1) * 2 * P], [
                            (tuple(vtile[:, part, j, :] if b else vshift[:, part, 4 * u + j, :]
                                   for part in range(2)),
                             (pT_hi[:, j % 2, b, :], pT_lo[:, j % 2, b, :]))])
                    last.then_inc(sem("pv_ready"), 1)

                def out_tile(k):
                    if not first:
                        outputs(i, c, k)

                pe.wait_ge(sem("qk_copied"), times(i, c, 5, 3))
                scores(0, 0)
                scores(1, 0)
                pe.wait_ge(sem("qk_copied"), times(i, c, 5, 5))
                scores(0, 1)
                scores(1, 1)
                out_tile(0)
                scores(2, 0)
                scores(2, 1)
                scores(3, 0)
                scores(3, 1)
                out_tile(1)
                if first:
                    values_of(i, c + 1)
                    keys_of(i, c + 1)
                probs_T(0)
                probs_T(1)
                out_tile(2)
                values(0)
                probs_T(2)
                values(1)
                if ahead:
                    out_tile(3)
                point("values1")
                probs_T(3)
                values(2)
                point("values2")
                if ahead and not first:
                    values_of(i, c + 1)
                values(3)
                point("values3")
                if not ahead:
                    out_tile(3)
                if ahead and not first:
                    keys_of(i, c + 1)

            def outputs(i, c, k):
                pe.wait_ge(sem("oT_split"), times(i, c - 1, 4, k + 1))
                if k == 0:
                    pe.wait_ge(sem("wo_split"), times(i, (c - 1) // 2 * 2, 2, 4))
                if k < 2:
                    if c < STEPS:
                        pe.wait_ge(sem("qk_copied"), times(i, c, 5, 4 + k))
                    else:
                        pe.wait_ge(sem("out_added"), times(i, c - 2, 4, 3 + k))
                else:
                    pe.wait_ge(sem("out_added"), times(i, c - 1, 4, k - 1))
                t = slice(k * P, k * P + P)
                product(ps_r[k % 2][:], [((oT_hi[:, h, t], oT_lo[:, h, t]), (wo_hi[:, h, :], wo_lo[:, h, :]))
                                         for h in range(GROUP)]).then_inc(sem("out_ready"), 1)

            def second_half(t):
                return {"keys": [(tile1, t + 4), (tile1, t + 5)], "query0": [(tile1, t + 6), (tile1, t + 7)]}

            def first_values_keys(c, tiles):
                pe.wait_ge(sem("xnT_split"), tiles)
                values_of(None, c)
                keys_of(None, c)

            pe.wait_ge(sem("ident_ready"), 1)
            for _ in range(WARM_UP):
                pe.transpose(ps_p[1][:, 0:P], ident[:], ident[:])
            for t in range(4):
                tile1(t)
            first_values_keys(0, 4)
            step(None, 0, True, extra=second_half(0))
            step(None, 1)
            with pe.Fori(0, N_KV - 2) as i:
                step(i, 2)
                step(i, 3)
            step(None, 2 * N_KV - 2)
            t = SEQ_TILES
            step(None, 2 * N_KV - 1, ahead=False, extra={
                "values1": [(tile1, t)], "values2": [(tile1, t + 1)],
                "values3": [(tile1, t + 2), (tile1, t + 3)]})
            first_values_keys(2 * N_KV, t + 4)
            step(None, 2 * N_KV, extra=second_half(t))
            step(None, 2 * N_KV + 1)
            with pe.Fori(0, N_KV - 2) as i:
                step(i, 2 * N_KV + 2)
                step(i, 2 * N_KV + 3)
            step(None, STEPS - 2)
            step(None, STEPS - 1, ahead=False, extra={"values2": [(tile2, 0)], "values3": [(tile2, 1)]})
            outputs(None, STEPS, 0)
            outputs(None, STEPS, 1)
            tile2(2)
            tile2(3)
            outputs(None, STEPS, 2)
            outputs(None, STEPS, 3)

            def gate_up(i, p, tb, t, m):
                n = 2 * tb + t
                toks = slice(STEP * (tb % 2), STEP * (tb % 2) + STEP)
                x_hi, x_lo = x2T[tb // 2]
                ps, ready, free = ((ps_s, "gate_ready", "silu_ready"), (ps_p, "up_ready", "h_ready"))[m]
                if n >= 2:
                    pe.wait_ge(sem(free), of_pair(i, p, 8, n - 1))
                product(ps[n % 2][:], [
                    ((wf_hi[:, t, m, k * P:k * P + P], wf_lo[:, t, m, k * P:k * P + P]),
                     (x_hi[:, k, toks], x_lo[:, k, toks])) for k in range(KC)]).then_inc(sem(ready), 1)

            def down(i, p):
                pe.wait_ge(sem("down_split"), of_pair(i, p, 2, 2))
                for t in range(TILES):
                    pe.wait_ge(sem("h_split"), of_pair(i, p, 8, 2 * (t // 4) + 2))
                    if t >= 2:
                        pe.wait_ge(sem("down_added"), of_pair(i, p, TILES, t - 1))
                    tt = slice(t * P, t * P + P)
                    product(ps_o[t % 2][:], [
                        ((hT_hi[:, a, tt], hT_lo[:, a, tt]), (wf_hi[:, a, 2, :], wf_lo[:, a, 2, :]))
                        for a in range(2)]).then_inc(sem("down_ready"), 1)

            pe.wait_ge(sem("gateup_split"), 4)
            for tb in range(4):
                pe.wait_ge(sem("xnT_split"), TILES + 4 * tb + 4)
                for t in range(2):
                    for m in range(2):
                        if tb < 3 and (t, m) != (0, 0):
                            for k in {(0, 1): (4,), (1, 0): (5,), (1, 1): (6, 7)}[t, m]:
                                if tb == 0 and k < 6:
                                    pe.wait_ge(sem("out_added"), 4 * STEPS - 1 + k % 2)
                                tile2(4 * tb + k)
                        gate_up(None, 0, tb, t, m)
            down(None, 0)
            with pe.Fori(0, PAIRS - 1) as i:
                pe.wait_ge(sem("gateup_split"), i * 4 + 8)
                for tb in range(4):
                    for t in range(2):
                        for m in range(2):
                            gate_up(i, 1, tb, t, m)
                down(i, 1)


def group(i, off):
    return i + off


def kernel(**inputs):
    import concourse.bacc as bacc
    from concourse.bass_utils import run_bass_kernel_spmd

    def by_chunk(w, rows, cols):
        return w.reshape(rows // P, P, cols).transpose(1, 0, 2).reshape(P, -1)

    a = {k: np.asarray(v) for k, v in inputs.items()}
    wq, wk, wv, wo = (a[f"L0_attn_w{k}"] for k in "qkvo")
    gd = GROUP * HD
    w_qkv = np.stack([np.concatenate([by_chunk(wv[g * HD:(g + 1) * HD].T, D, HD),
                                      by_chunk(wk[g * HD:(g + 1) * HD].T, D, HD),
                                      by_chunk(wq[g * gd:(g + 1) * gd].T, D, gd)], 1) for g in range(N_KV)])
    w_o = np.stack([by_chunk(wo.T[g * gd:(g + 1) * gd], gd, D) for g in range(N_KV)])
    codes, scales = [], []
    gq, uq, dq = (a[f"L0_ffn_{k}_q"] for k in ("gate", "up", "down"))
    ga, ua = (a[f"L0_ffn_{k}_absmax"].reshape(M_FFN, D // 64) for k in ("gate", "up"))
    da = a["L0_ffn_down_absmax"].reshape(D, M_FFN // 64)
    for t in range(MT):
        m = slice(t * P, t * P + P)
        codes.append(np.concatenate([by_chunk(gq[m].T, D, P), by_chunk(uq[m].T, D, P), dq[:, m].T], 1))
        scales.append(np.concatenate([ga[m].T.reshape(KC, 2, P).transpose(1, 0, 2).reshape(2, -1),
                                      ua[m].T.reshape(KC, 2, P).transpose(1, 0, 2).reshape(2, -1),
                                      da[:, 2 * t:2 * t + 2].T], 1))
    arrays = {"x": a["L0_attn_x"].reshape(BATCH * SEQ, D), "w_qkv": w_qkv, "w_o": w_o,
              "codes": np.stack(codes), "absmax": np.stack(scales)}
    arrays = {f"{k}_dram": np.ascontiguousarray(v) for k, v in arrays.items()}

    nc = bacc.Bacc("TRN2", target_bir_lowering=False, num_devices=1)
    args = [nc.dram_tensor(k, v.shape, mybir.dt.from_np(v.dtype), kind="ExternalInput").ap()
            for k, v in arrays.items()]
    out = nc.dram_tensor("out_dram", (BATCH * SEQ, D), F32, kind="ExternalOutput").ap()
    build(nc, *args, out)
    r = run_bass_kernel_spmd(nc, [arrays], core_ids=[0])
    return r.results[0]["out_dram"].reshape(BATCH, SEQ, D)
```
